# Optimizing a Trainium2 kernel written in Bass

```python
import numpy as np
import jax
import jax.numpy as jnp

def _softmax(x, axis=-1):
    return jax.nn.softmax(x, axis=axis)

def _gelu(x):
    return jax.nn.gelu(x, approximate=True)

def _silu(x):
    return jax.nn.silu(x)

def _sigmoid(x):
    return jax.nn.sigmoid(x)

def _layernorm(x, axis=-1, eps=1e-05):
    m = jnp.mean(x, axis=axis, keepdims=True)
    v = jnp.var(x, axis=axis, keepdims=True)
    return (x - m) / jnp.sqrt(v + eps)

def _scatter_add(tgt, idx, src, axis=0):
    return tgt.at[idx].add(src)

def _segment_sum(src, seg, n):
    return jax.ops.segment_sum(src, seg, n)
kernel_name = 'mk_dlrm_tower_d1_rec_r8_8b07ad'

def setup_inputs(seed: int=0):
    np.random.seed(seed)
    _w = jnp.asarray

    def _rec_inputs():
        import jax
        import jax.numpy as jnp
        _tk = jax.random.key(seed)
        dense_ctx = jax.random.normal(jax.random.fold_in(_tk, 190), (2048, 16), jnp.float32)
        ids = jnp.stack([jax.random.randint(jax.random.fold_in(_tk, 200 + f), (2048,), 0, v, jnp.int32) for f, v in enumerate([12500, 1250, 125000, 1000, 125000, 12500, 12500, 1250, 1250, 1000, 1000, 1000, 1000, 1250, 1250, 1000, 125000, 12500, 1250, 1250, 12500, 125000, 125000, 1000, 1250, 1000, 1000, 1000, 1000, 12500, 12500, 1000, 1000, 12500, 125000, 125000, 1250, 1000, 125000])], axis=1)
        tbl_0 = 0.05 * jax.random.normal(jax.random.fold_in(_tk, 500 + 0), (12500, 16), jnp.float32)
        tbl_1 = 0.05 * jax.random.normal(jax.random.fold_in(_tk, 500 + 1), (1250, 16), jnp.float32)
        tbl_2 = 0.05 * jax.random.normal(jax.random.fold_in(_tk, 500 + 2), (125000, 16), jnp.float32)
        tbl_3 = 0.05 * jax.random.normal(jax.random.fold_in(_tk, 500 + 3), (1000, 16), jnp.float32)
        tbl_4 = 0.05 * jax.random.normal(jax.random.fold_in(_tk, 500 + 4), (125000, 16), jnp.float32)
        tbl_5 = 0.05 * jax.random.normal(jax.random.fold_in(_tk, 500 + 5), (12500, 16), jnp.float32)
        tbl_6 = 0.05 * jax.random.normal(jax.random.fold_in(_tk, 500 + 6), (12500, 16), jnp.float32)
        tbl_7 = 0.05 * jax.random.normal(jax.random.fold_in(_tk, 500 + 7), (1250, 16), jnp.float32)
        tbl_8 = 0.05 * jax.random.normal(jax.random.fold_in(_tk, 500 + 8), (1250, 16), jnp.float32)
        tbl_9 = 0.05 * jax.random.normal(jax.random.fold_in(_tk, 500 + 9), (1000, 16), jnp.float32)
        tbl_10 = 0.05 * jax.random.normal(jax.random.fold_in(_tk, 500 + 10), (1000, 16), jnp.float32)
        tbl_11 = 0.05 * jax.random.normal(jax.random.fold_in(_tk, 500 + 11), (1000, 16), jnp.float32)
        tbl_12 = 0.05 * jax.random.normal(jax.random.fold_in(_tk, 500 + 12), (1000, 16), jnp.float32)
        tbl_13 = 0.05 * jax.random.normal(jax.random.fold_in(_tk, 500 + 13), (1250, 16), jnp.float32)
        tbl_14 = 0.05 * jax.random.normal(jax.random.fold_in(_tk, 500 + 14), (1250, 16), jnp.float32)
        tbl_15 = 0.05 * jax.random.normal(jax.random.fold_in(_tk, 500 + 15), (1000, 16), jnp.float32)
        tbl_16 = 0.05 * jax.random.normal(jax.random.fold_in(_tk, 500 + 16), (125000, 16), jnp.float32)
        tbl_17 = 0.05 * jax.random.normal(jax.random.fold_in(_tk, 500 + 17), (12500, 16), jnp.float32)
        tbl_18 = 0.05 * jax.random.normal(jax.random.fold_in(_tk, 500 + 18), (1250, 16), jnp.float32)
        tbl_19 = 0.05 * jax.random.normal(jax.random.fold_in(_tk, 500 + 19), (1250, 16), jnp.float32)
        tbl_20 = 0.05 * jax.random.normal(jax.random.fold_in(_tk, 500 + 20), (12500, 16), jnp.float32)
        tbl_21 = 0.05 * jax.random.normal(jax.random.fold_in(_tk, 500 + 21), (125000, 16), jnp.float32)
        tbl_22 = 0.05 * jax.random.normal(jax.random.fold_in(_tk, 500 + 22), (125000, 16), jnp.float32)
        tbl_23 = 0.05 * jax.random.normal(jax.random.fold_in(_tk, 500 + 23), (1000, 16), jnp.float32)
        tbl_24 = 0.05 * jax.random.normal(jax.random.fold_in(_tk, 500 + 24), (1250, 16), jnp.float32)
        tbl_25 = 0.05 * jax.random.normal(jax.random.fold_in(_tk, 500 + 25), (1000, 16), jnp.float32)
        tbl_26 = 0.05 * jax.random.normal(jax.random.fold_in(_tk, 500 + 26), (1000, 16), jnp.float32)
        tbl_27 = 0.05 * jax.random.normal(jax.random.fold_in(_tk, 500 + 27), (1000, 16), jnp.float32)
        tbl_28 = 0.05 * jax.random.normal(jax.random.fold_in(_tk, 500 + 28), (1000, 16), jnp.float32)
        tbl_29 = 0.05 * jax.random.normal(jax.random.fold_in(_tk, 500 + 29), (12500, 16), jnp.float32)
        tbl_30 = 0.05 * jax.random.normal(jax.random.fold_in(_tk, 500 + 30), (12500, 16), jnp.float32)
        tbl_31 = 0.05 * jax.random.normal(jax.random.fold_in(_tk, 500 + 31), (1000, 16), jnp.float32)
        tbl_32 = 0.05 * jax.random.normal(jax.random.fold_in(_tk, 500 + 32), (1000, 16), jnp.float32)
        tbl_33 = 0.05 * jax.random.normal(jax.random.fold_in(_tk, 500 + 33), (12500, 16), jnp.float32)
        tbl_34 = 0.05 * jax.random.normal(jax.random.fold_in(_tk, 500 + 34), (125000, 16), jnp.float32)
        tbl_35 = 0.05 * jax.random.normal(jax.random.fold_in(_tk, 500 + 35), (125000, 16), jnp.float32)
        tbl_36 = 0.05 * jax.random.normal(jax.random.fold_in(_tk, 500 + 36), (1250, 16), jnp.float32)
        tbl_37 = 0.05 * jax.random.normal(jax.random.fold_in(_tk, 500 + 37), (1000, 16), jnp.float32)
        tbl_38 = 0.05 * jax.random.normal(jax.random.fold_in(_tk, 500 + 38), (125000, 16), jnp.float32)
        _rk = jax.random.fold_in(_tk, 7)
        W_top1 = 0.0606339 * jax.random.normal(jax.random.fold_in(_tk, 801), (272, 512), jnp.float32)
        W_top2 = 0.0441942 * jax.random.normal(jax.random.fold_in(_tk, 802), (512, 256), jnp.float32)
        W_top3 = 0.0625 * jax.random.normal(jax.random.fold_in(_tk, 803), (256, 1), jnp.float32)
        b_top1 = jnp.zeros((512,), jnp.float32)
        b_top2 = jnp.zeros((256,), jnp.float32)
        return (dense_ctx, ids, tbl_0, tbl_1, tbl_2, tbl_3, tbl_4, tbl_5, tbl_6, tbl_7, tbl_8, tbl_9, tbl_10, tbl_11, tbl_12, tbl_13, tbl_14, tbl_15, tbl_16, tbl_17, tbl_18, tbl_19, tbl_20, tbl_21, tbl_22, tbl_23, tbl_24, tbl_25, tbl_26, tbl_27, tbl_28, tbl_29, tbl_30, tbl_31, tbl_32, tbl_33, tbl_34, tbl_35, tbl_36, tbl_37, tbl_38, W_top1, b_top1, W_top2, b_top2, W_top3)
    dense_ctx, ids, tbl_0, tbl_1, tbl_2, tbl_3, tbl_4, tbl_5, tbl_6, tbl_7, tbl_8, tbl_9, tbl_10, tbl_11, tbl_12, tbl_13, tbl_14, tbl_15, tbl_16, tbl_17, tbl_18, tbl_19, tbl_20, tbl_21, tbl_22, tbl_23, tbl_24, tbl_25, tbl_26, tbl_27, tbl_28, tbl_29, tbl_30, tbl_31, tbl_32, tbl_33, tbl_34, tbl_35, tbl_36, tbl_37, tbl_38, W_top1, b_top1, W_top2, b_top2, W_top3 = _rec_inputs()

    def _L0_rec_setup():
        import jax, jax.numpy as jnp
        import numpy as np
        B, F0, D = (256, 39, 16)
        LAYER_SIZES = [128, 128, 128]
        key = jax.random.key(seed)
        ks = jax.random.split(key, 1 + 2 * len(LAYER_SIZES))
        inputs = jax.random.normal(ks[0], (B, F0, D), dtype=jnp.float32)
        out = {'inputs': inputs}
        field_nums = [F0]
        for i, size in enumerate(LAYER_SIZES):
            fk = field_nums[-1]
            fan_in = F0 * fk
            scale = np.sqrt(2.0 / (fan_in + size)).astype(np.float32)
            out[f'w{i}'] = jax.random.normal(ks[1 + 2 * i], (F0, fk, size), dtype=jnp.float32) * scale
            out[f'b{i}'] = jnp.zeros((size,), dtype=jnp.float32)
            field_nums.append(size // 2)
        return out
    _L0_rec_all = _L0_rec_setup()
    _L0_rec_in = {k: v for k, v in _L0_rec_all.items() if k in ('w0', 'w1', 'w2', 'b0', 'b1', 'b2')}
    del _L0_rec_all
    return {'dense_ctx': dense_ctx, 'ids': ids, 'tbl_0': tbl_0, 'tbl_1': tbl_1, 'tbl_2': tbl_2, 'tbl_3': tbl_3, 'tbl_4': tbl_4, 'tbl_5': tbl_5, 'tbl_6': tbl_6, 'tbl_7': tbl_7, 'tbl_8': tbl_8, 'tbl_9': tbl_9, 'tbl_10': tbl_10, 'tbl_11': tbl_11, 'tbl_12': tbl_12, 'tbl_13': tbl_13, 'tbl_14': tbl_14, 'tbl_15': tbl_15, 'tbl_16': tbl_16, 'tbl_17': tbl_17, 'tbl_18': tbl_18, 'tbl_19': tbl_19, 'tbl_20': tbl_20, 'tbl_21': tbl_21, 'tbl_22': tbl_22, 'tbl_23': tbl_23, 'tbl_24': tbl_24, 'tbl_25': tbl_25, 'tbl_26': tbl_26, 'tbl_27': tbl_27, 'tbl_28': tbl_28, 'tbl_29': tbl_29, 'tbl_30': tbl_30, 'tbl_31': tbl_31, 'tbl_32': tbl_32, 'tbl_33': tbl_33, 'tbl_34': tbl_34, 'tbl_35': tbl_35, 'tbl_36': tbl_36, 'tbl_37': tbl_37, 'tbl_38': tbl_38, 'W_top1': W_top1, 'b_top1': b_top1, 'W_top2': W_top2, 'b_top2': b_top2, 'W_top3': W_top3, 'L0_rec_w0': _L0_rec_in['w0'], 'L0_rec_w1': _L0_rec_in['w1'], 'L0_rec_w2': _L0_rec_in['w2'], 'L0_rec_b0': _L0_rec_in['b0'], 'L0_rec_b1': _L0_rec_in['b1'], 'L0_rec_b2': _L0_rec_in['b2']}

def reference(dense_ctx, ids, tbl_0, tbl_1, tbl_2, tbl_3, tbl_4, tbl_5, tbl_6, tbl_7, tbl_8, tbl_9, tbl_10, tbl_11, tbl_12, tbl_13, tbl_14, tbl_15, tbl_16, tbl_17, tbl_18, tbl_19, tbl_20, tbl_21, tbl_22, tbl_23, tbl_24, tbl_25, tbl_26, tbl_27, tbl_28, tbl_29, tbl_30, tbl_31, tbl_32, tbl_33, tbl_34, tbl_35, tbl_36, tbl_37, tbl_38, W_top1, b_top1, W_top2, b_top2, W_top3, L0_rec_w0, L0_rec_w1, L0_rec_w2, L0_rec_b0, L0_rec_b1, L0_rec_b2):
    import jax
    import jax.numpy as jnp

    def _L0_rec_ref(inputs, w0, w1, w2, b0, b1, b2):
        import jax, jax.numpy as jnp
        import numpy as np
        B, F0, D = (256, 39, 16)
        LAYER_SIZES = [128, 128, 128]
        x0 = inputs
        xk = inputs
        params = [(w0, b0), (w1, b1), (w2, b2)]
        n_layers = len(params)
        direct = []
        for idx, (W, b) in enumerate(params):
            z = jnp.einsum('bhd,bkd,hks->bsd', x0, xk, W) + b[None, :, None]
            z = jax.nn.relu(z)
            if idx != n_layers - 1:
                half = z.shape[1] // 2
                xk = z[:, :half, :]
                direct.append(z[:, half:, :])
            else:
                direct.append(z)
        logit = jnp.sum(jnp.concatenate(direct, axis=1), axis=-1)
        return logit
    e = jnp.stack([tbl_0[ids[:, 0]], tbl_1[ids[:, 1]], tbl_2[ids[:, 2]], tbl_3[ids[:, 3]], tbl_4[ids[:, 4]], tbl_5[ids[:, 5]], tbl_6[ids[:, 6]], tbl_7[ids[:, 7]], tbl_8[ids[:, 8]], tbl_9[ids[:, 9]], tbl_10[ids[:, 10]], tbl_11[ids[:, 11]], tbl_12[ids[:, 12]], tbl_13[ids[:, 13]], tbl_14[ids[:, 14]], tbl_15[ids[:, 15]], tbl_16[ids[:, 16]], tbl_17[ids[:, 17]], tbl_18[ids[:, 18]], tbl_19[ids[:, 19]], tbl_20[ids[:, 20]], tbl_21[ids[:, 21]], tbl_22[ids[:, 22]], tbl_23[ids[:, 23]], tbl_24[ids[:, 24]], tbl_25[ids[:, 25]], tbl_26[ids[:, 26]], tbl_27[ids[:, 27]], tbl_28[ids[:, 28]], tbl_29[ids[:, 29]], tbl_30[ids[:, 30]], tbl_31[ids[:, 31]], tbl_32[ids[:, 32]], tbl_33[ids[:, 33]], tbl_34[ids[:, 34]], tbl_35[ids[:, 35]], tbl_36[ids[:, 36]], tbl_37[ids[:, 37]], tbl_38[ids[:, 38]]], axis=1)
    z = _L0_rec_ref(e, L0_rec_w0, L0_rec_w1, L0_rec_w2, L0_rec_b0, L0_rec_b1, L0_rec_b2)
    z = z.reshape(z.shape[0], -1)
    h = jnp.concatenate([z, dense_ctx], axis=1)
    h = jnp.maximum(h @ W_top1 + b_top1, 0.0)
    h = jnp.maximum(h @ W_top2 + b_top2, 0.0)
    y = h @ W_top3
    return y

_drawn_inputs = setup_inputs


def setup_inputs(seed=0):
    import zlib

    import numpy as np

    out = dict(_drawn_inputs(seed))
    spreads = {'b_top1': (0.0, 2.0),
     'b_top2': (0.0, 2.0),
     'L0_rec_b0': (0.0, 0.343),
     'L0_rec_b1': (0.0, 0.524),
     'L0_rec_b2': (0.0, 0.8)}
    factors = {'tbl_0': 8.0,
     'tbl_1': 8.0,
     'tbl_2': 8.0,
     'tbl_3': 8.0,
     'tbl_4': 8.0,
     'tbl_5': 8.0,
     'tbl_6': 8.0,
     'tbl_7': 8.0,
     'tbl_8': 8.0,
     'tbl_9': 8.0,
     'tbl_10': 8.0,
     'tbl_11': 8.0,
     'tbl_12': 8.0,
     'tbl_13': 8.0,
     'tbl_14': 8.0,
     'tbl_15': 8.0,
     'tbl_16': 8.0,
     'tbl_17': 8.0,
     'tbl_18': 8.0,
     'tbl_19': 8.0,
     'tbl_20': 8.0,
     'tbl_21': 8.0,
     'tbl_22': 8.0,
     'tbl_23': 8.0,
     'tbl_24': 8.0,
     'tbl_25': 8.0,
     'tbl_26': 8.0,
     'tbl_27': 8.0,
     'tbl_28': 8.0,
     'tbl_29': 8.0,
     'tbl_30': 8.0,
     'tbl_31': 8.0,
     'tbl_32': 8.0,
     'tbl_33': 8.0,
     'tbl_34': 8.0,
     'tbl_35': 8.0,
     'tbl_36': 8.0,
     'tbl_37': 8.0,
     'tbl_38': 8.0,
     'L0_rec_w0': 8.0,
     'L0_rec_w1': 6.252,
     'L0_rec_w2': 4.773,
     'dense_ctx': 8.0}
    for name, (base, spread) in spreads.items():
        noise = np.random.default_rng([zlib.crc32(name.encode()), seed]).standard_normal(out[name].shape)
        drawn = base * np.exp(spread * noise) if base else spread * noise
        out[name] = jnp.asarray(drawn.astype(out[name].dtype))
    for name, factor in factors.items():
        out[name] = (out[name] * factor).astype(out[name].dtype)
    return out
```

```python
import concourse.bass as bass
from concourse import mybir
from contextlib import ExitStack

F32 = mybir.dt.float32
I32 = mybir.dt.int32
F32R = mybir.dt.float32r
ALU = mybir.AluOpType
ACT = mybir.ActivationFunctionType
AXIS = mybir.AxisListType

B, F, D, P = 2048, 39, 16, 128
S = 128
HALF = S // 2
GROUPS = B // P
CHUNKS = 4
CB = P // CHUNKS
N = CB * D
DIAG = 3
T0 = 7
R0 = DIAG * F
R0_LAST = 2 * F
TX = 20
WRAP = 20
RING = 6
SL0, SLX = (T0 + 1) // 2, TX // 2
SLC = SL0 + 2 * SLX
COLS = B * D
HALF_SLOT = 2
SPLIT_SLOTS = (1, 4, 7)
SPLIT_RING = 2
assert all(b - a >= RING for a, b in zip(SPLIT_SLOTS, SPLIT_SLOTS[SPLIT_RING:]))
SLOT_TILES = [(2 * k, 2 * k + 1) for k in range(SLX - 1)]
SLOT_TILES.insert(HALF_SLOT, (TX - 2, TX - 1))
SPLIT_TILES = [t for k in SPLIT_SLOTS for t in SLOT_TILES[k]]
PLAIN_TILES = [t for t in range(TX - 1) if t not in SPLIT_TILES]
SPLITS = len(SPLIT_TILES) + 1
ROUNDED_SLOTS = sorted((HALF_SLOT,) + SPLIT_SLOTS)
ROUNDED = len(ROUNDED_SLOTS)
EARLY = sum(k < RING for k in ROUNDED_SLOTS)
SUB_LAG = 2
X0_DIAG_DMAS, X0_PAIRS_DMAS, ST_DMAS = 2 * DIAG, 3, 4
RAW_DMAS, WEIGHT_DMAS, TOP_DMAS = 4, 8, 6
H1, H2, DENSE = 512, 256, 16
NB = 512


def top_order():
    steps = []
    for n in range(B // NB + 1):
        if n < B // NB:
            steps += [("h1", n, m) for m in range(H1 // P)]
        if n > 0:
            steps += [("h2", n - 1, m) for m in range(H2 // P)] + [("y", n - 1, 0)]
    return steps


TOP_ORDER = top_order()
TOP_STEPS = len(TOP_ORDER)


def last_h1(n):
    return TOP_ORDER.index(("h1", n, H1 // P - 1)) + 1


def build(nc, tables, ids, dense_t, w0f, w0s, w1, w2, b0, b1, b2, wt1, bt1, wt2, bt2, wt3, out):
    xt = nc.dram_tensor("x0_transposed", [F + WRAP, COLS], F32, kind="Internal").ap()

    ctx = ExitStack()
    with ctx:
        def sb(name, shape, dt=F32):
            return ctx.enter_context(nc.sbuf_tensor(name, shape, dt))

        def ps(name):
            return ctx.enter_context(nc.psum_tensor(name, [P, N], F32))

        def sem(name):
            return ctx.enter_context(nc.semaphore(name))

        x0_pairs = [sb(f"x0_pairs{i}", [P, TX, N]) for i in range(2)]
        x0_diag = sb("x0_diag", [P, T0 + 1, N])
        prod = sb("prod", [P, RING, 2, N])
        prod_hi = sb("prod_hi", [P, SPLIT_RING, 2, N], F32R)
        prod_lo = sb("prod_lo", [P, SPLIT_RING, 2, N], F32R)
        half_parts = sb("half_parts", [P, N], F32R)
        xk1 = sb("xk1", [P, N])
        xk2 = sb("xk2", [P, N])
        direct01 = sb("direct01", [P, N])
        direct2 = sb("direct2", [P, N])
        logit01 = sb("logit01", [P, B])
        logit2 = sb("logit2", [P, CB + B])
        idx = sb("idx", [P, F], I32)
        emb = sb("emb", [P, F * D])
        stage = sb("stage", [P, CHUNKS, D // 2, CB])
        ident = sb("ident", [P, P])
        w0_sb = sb("w0_sb", [P, T0, S])
        w_plain = [sb(f"w{n}_plain", [P, len(PLAIN_TILES), S]) for n in (1, 2)]
        w_hi = [sb(f"w{n}_hi", [P, SPLITS, S], F32R) for n in (1, 2)]
        w_lo = [sb(f"w{n}_lo", [P, SPLITS, S], F32R) for n in (1, 2)]
        wt3_sb = sb("wt3_sb", [P, H2 // P])
        b0_sb = sb("b0_sb", [P, 1])
        b1_sb = sb("b1_sb", [P, 1])
        b2_sb = sb("b2_sb", [P, 1])
        bt1_sb = sb("bt1_sb", [P, H1 // P])
        bt2_sb = sb("bt2_sb", [P, H2 // P])
        w0_swapped = x0_pairs[1][0:R0, 0:2, :].rearrange("p a n -> p (a n)")[:, 0:T0 * S]
        w_raw = [x0_pairs[1][:, 2 + 2 * i:4 + 2 * i, :].rearrange("p a n -> p (a n)")[:, 0:SPLITS * S]
                 for i in range(2)]
        def top_part(first, n):
            return x0_pairs[0][:, first:first + n, :].rearrange("p a n -> p (a n)")

        wt1a_sb, wt1b_sb, wt1c_sb = top_part(0, 1), top_part(1, 1), top_part(2, 1)[0:DENSE]
        wt2_sb = top_part(3, 2).rearrange("p (t n) -> p t n", n=H2)
        dense_sb = top_part(5, 4)[0:DENSE]
        h2_sb = top_part(9, 4).rearrange("p (i m n) -> p i m n", i=2, n=NB)
        y_sb = top_part(13, 4)[0:1]
        h1_sb = x0_diag[:].rearrange("p (i m) n -> p i m n", i=2)

        z = [ps("z0"), ps("z1"), ps("z2")]
        turned = [ps("turned0"), ps("turned1")]
        top = z + [ps("top0"), ps("top1"), ps("top2")]

        swapped_in = sem("swapped_in")
        raw_in = sem("raw_in")
        w0_summed = sem("w0_summed")
        w_hi_ready = sem("w_hi_ready")
        w_split = sem("w_split")
        weights_in = sem("weights_in")
        top_weights_in = sem("top_weights_in")
        ident_zero = sem("ident_zero")
        ident_ready = sem("ident_ready")
        idx_in = sem("idx_in")
        gather_started = sem("gather_started")
        gathered = sem("gathered")
        turned_ready = sem("turned_ready")
        stage_ready = sem("stage_ready")
        xt_stored = sem("xt_stored")
        x0_diag_in = sem("x0_diag_in")
        x0_pairs_in = [sem(f"x0_pairs_in{i}") for i in range(2)]
        prod_ready = sem("prod_ready")
        hi_ready = sem("hi_ready")
        lo_ready = sem("lo_ready")
        slot_free = sem("slot_free")
        xk_ready = [sem("xk1_ready"), sem("xk2_ready")]
        direct01_ready = sem("direct01_ready")
        direct2_ready = sem("direct2_ready")
        summed01 = sem("summed01")
        summed2 = sem("summed2")
        h_ready = sem("h_ready")
        h_relu = sem("h_relu")
        y_stored = sem("y_stored")

        block = ctx.enter_context(nc.Block())

        @block.sync
        def _(sp):
            sp.dma_start(w0_swapped, w0s).then_inc(swapped_in, 16)
            sp.dma_start(w0_sb[0:R0].rearrange("p t s -> p (t s)"), w0f).then_inc(swapped_in, 16)
            plain = len(PLAIN_TILES)
            for n, w in enumerate((w1, w2)):
                raw = w_raw[n].rearrange("p (t s) -> p t s", s=S)
                sp.dma_start(raw[:, 0:SPLITS - 1], w[:, plain:plain + SPLITS - 1]).then_inc(raw_in, 16)
                sp.dma_start(raw[:, SPLITS - 1], w[:, TX - 1]).then_inc(raw_in, 16)
            loads = [(w_plain[0][:], w1[:, 0:plain]), (w_plain[1][:], w2[:, 0:plain]),
                     (b0_sb[:], b0), (b1_sb[:], b1), (b2_sb[:], b2),
                     (bt1_sb[:], bt1), (bt2_sb[:], bt2), (wt3_sb[:], wt3)]
            assert len(loads) == WEIGHT_DMAS
            for dst, src in loads:
                sp.dma_start(dst, src).then_inc(weights_in, 16)

            slots_done = sp.alloc_register("slots_done")

            def ahead(value):
                return value if isinstance(value, int) else sp.snap(value)

            def store_group(bt):
                first = ahead(bt * (P * D))
                sp.wait_ge(stage_ready, 2 * (bt + 1))
                cols = xt[:, bass.ds(first, P * D)].rearrange(
                    "f (c e n) -> f c e n", c=CHUNKS, e=2)
                for half in range(2):
                    src = stage[half:2 * F:2].rearrange("p c d b -> p c (d b)")
                    sp.dma_start(cols[0:F, :, half, :], src).then_inc(xt_stored, 16)
                    sp.dma_start(cols[F:F + WRAP, :, half, :], src[0:WRAP]).then_inc(xt_stored, 16)

            def load_chunk(bt, c):
                first = ahead(bt * (P * D) + c * N)
                slots = (bt * CHUNKS + c) * SLC - SLC + SL0 + 1
                if not isinstance(bt, int):
                    sp.reg_mov(slots_done, slots)
                    slots = slots_done
                if c == 0:
                    sp.wait_ge(xt_stored, 16 * ST_DMAS * (bt + 1))
                if not (isinstance(bt, int) and bt == c == 0):
                    sp.wait_ge(prod_ready, slots)
                chunk = xt[:, bass.ds(first, N)]
                for i in range(DIAG):
                    rows = slice(i * F, (i + 1) * F)
                    shifted = bass.AP(tensor=chunk.tensor, offset=chunk[i:i + F].offset,
                                      ap=[[COLS, F], [DIAG * COLS, T0], [1, N]])
                    sp.dma_start(x0_diag[rows, 0:T0, :], shifted).then_inc(x0_diag_in, 16)
                    sp.dma_start(x0_diag[rows, T0, :], chunk[0:F]).then_inc(x0_diag_in, 16)
                buf, loaded = x0_pairs[c % 2], x0_pairs_in[c % 2]
                for half in range(2):
                    src = chunk[half:half + F - 1].rearrange("(t two) n -> t two n", two=2)[:, 0, :]
                    sp.dma_start(buf[half * HALF:(half + 1) * HALF, 0:TX - 1, :],
                                 src.partition_broadcast(HALF)).then_inc(loaded, 16)
                src = chunk[F - 1:F].rearrange("o n -> (o n)")
                sp.dma_start(buf[:, TX - 1, :], src.partition_broadcast(P)).then_inc(loaded, 16)

            def load_top():
                sp.wait_ge(prod_ready, (GROUPS * CHUNKS - 1) * SLC + SL0 + 1)
                loads = [
                    (wt1a_sb[0:HALF], wt1[HALF:P]), (wt1a_sb[HALF:P], wt1[0:HALF]),
                    (wt1b_sb, wt1[P:2 * P]), (wt1c_sb, wt1[2 * P:2 * P + DENSE]),
                    (wt2_sb, wt2.rearrange("(t p) n -> p t n", p=P)), (dense_sb, dense_t),
                ]
                assert len(loads) == TOP_DMAS
                for dst, src in loads:
                    sp.dma_start(dst, src).then_inc(top_weights_in, 16)

            store_group(0)
            sp.wait_ge(w0_summed, 1)
            sp.wait_ge(w_split, 2)
            load_chunk(0, 0)

            def group(bt, last):
                for c in range(CHUNKS):
                    if c == 2 and not last:
                        store_group(bt + 1)
                    if c < CHUNKS - 1:
                        load_chunk(bt, c + 1)
                    elif not last:
                        load_chunk(bt + 1, 0)
                    else:
                        load_top()

            with sp.Fori(0, GROUPS - 1) as bt:
                group(bt, False)
            group(GROUPS - 1, True)
            sp.wait_ge(h_relu, TOP_STEPS)
            sp.dma_start(out, y_sb).then_inc(y_stored, 16)
            sp.wait_ge(y_stored, 16)

        @block.gpsimd
        def _(pool):
            nc.gpsimd.memset(ident[:], 0.0).then_inc(ident_zero, 1)
            pool.wait_ge(ident_zero, 1)
            nc.gpsimd.affine_select(out=ident[:], in_=ident[:], compare_op=ALU.not_equal, fill=1.0,
                                    base=0, pattern=[[-1, P]], channel_multiplier=1
                                    ).then_inc(ident_ready, 1)

            def gather(bt, first):
                if not first:
                    pool.wait_ge(gathered, 16 * F * bt)
                    pool.sem_inc(gather_started, 1)
                pool.dma_start(idx[:], ids[bass.ds(bt * P, P), :]).then_inc(idx_in, 16)
                pool.wait_ge(idx_in, 16 * (bt + 1))
                if not first:
                    pool.wait_ge(turned_ready, 2 * bt)
                pool.sem_inc(gather_started, 1)
                for f in range(F):
                    nc.gpsimd.indirect_dma_start(
                        out=emb[:, f * D:(f + 1) * D], out_offset=None, in_=tables[f],
                        in_offset=bass.IndirectOffsetOnAxis(ap=idx[:, f:f + 1], axis=0),
                    ).then_inc(gathered, 16)

            gather(0, True)
            with pool.Fori(1, GROUPS) as bt:
                gather(bt, False)

        @block.vector
        def _(dve):
            nc.vector.memset(z[2][:], 0.0).then_inc(summed2, 1)
            dve.sem_inc(slot_free, RING)
            dve.wait_ge(swapped_in, 32)
            w0 = w0_sb[0:R0].rearrange("p t s -> p (t s)")
            nc.vector.tensor_tensor(w0, w0, w0_swapped, ALU.add).then_inc(w0_summed, 1)
            for n in range(2):
                dve.wait_ge(w_hi_ready, n + 1)
                nc.vector.tensor_tensor(w_lo[n][:].rearrange("p t s -> p (t s)"), w_raw[n],
                                        w_hi[n][:].bitcast(F32).rearrange("p t s -> p (t s)"),
                                        ALU.subtract).then_inc(w_split, 1)

            def product(slot, pos, a, xk):
                rows, n = a.shape[0], a.shape[1]
                dve.wait_ge(slot_free, slot + 1)
                nc.vector.tensor_tensor(prod[0:rows, pos % RING, 0:n, :], a,
                                        xk.unsqueeze(1).broadcast_to([rows, n, N]),
                                        ALU.mult).then_inc(prod_ready, 1)

            def layer0(slot, pos, chunk):
                dve.wait_ge(x0_diag_in, 16 * X0_DIAG_DMAS * (chunk + 1))
                for k in range(SL0):
                    n = min(2, T0 - 2 * k)
                    product(slot + k, pos + k, x0_diag[0:R0, 2 * k:2 * k + n, :],
                            x0_diag[0:R0, T0, :])

            def low_parts(k, pos, split, layer, chunk):
                dve.wait_ge(hi_ready, (chunk * 2 + layer - 1) * ROUNDED + ROUNDED_SLOTS.index(k) + 1)
                held = prod[:, pos % RING]
                if k == HALF_SLOT:
                    nc.vector.tensor_tensor(half_parts[HALF:P], held[HALF:P, 1, :],
                                            half_parts[HALF:P].bitcast(F32),
                                            ALU.subtract).then_inc(lo_ready, 1)
                else:
                    nc.vector.tensor_tensor(prod_lo[:, split % SPLIT_RING], held,
                                            prod_hi[:, split % SPLIT_RING].bitcast(F32),
                                            ALU.subtract).then_inc(lo_ready, 1)

            def layer(n, slot, pos, split, copies, xk, chunk, sums_at, sums):
                for k in range(SLX + SUB_LAG):
                    if k < SLX:
                        t = SLOT_TILES[k][0]
                        product(slot + k, pos + k, copies[:, t:t + 2, :], xk[:])
                    if k - SUB_LAG in ROUNDED_SLOTS:
                        low_parts(k - SUB_LAG, pos + k - SUB_LAG, split, n, chunk)
                        split += k - SUB_LAG in SPLIT_SLOTS
                    if k == sums_at:
                        sums()
                return split

            def sum01(chunk):
                dve.wait_ge(direct01_ready, 2 * chunk + 2)
                nc.vector.tensor_reduce(logit01[:, bass.ds(chunk * CB, CB)],
                                        direct01[:].rearrange("p (d b) -> p b d", b=CB),
                                        AXIS.X, ALU.add).then_inc(summed01, 1)

            def sum2(chunk):
                dve.wait_ge(direct2_ready, chunk + 1)
                nc.vector.tensor_reduce(logit2[:, bass.ds(chunk * CB, CB)],
                                        direct2[:].rearrange("p (d b) -> p b d", b=CB),
                                        AXIS.X, ALU.add).then_inc(summed2, 1)

            layer0(0, 0, 0)

            def group(bt, last):
                split = 0
                for c in range(CHUNKS):
                    chunk = bt * CHUNKS + c
                    slot, pos = SL0 + chunk * SLC, SL0 + c * SLC
                    copies = x0_pairs[c % 2]
                    dve.wait_ge(x0_pairs_in[c % 2],
                                16 * X0_PAIRS_DMAS * (bt * (CHUNKS // 2) + c // 2 + 1))
                    dve.wait_ge(xk_ready[0], chunk + 1)
                    split = layer(1, slot, pos, split, copies, xk1, chunk, 8, lambda: sum2(chunk))
                    slot, pos = slot + SLX, pos + SLX
                    if not (last and c == CHUNKS - 1):
                        layer0(slot, pos, chunk + 1)
                        slot, pos = slot + SL0, pos + SL0
                    dve.wait_ge(xk_ready[1], chunk + 1)
                    split = layer(2, slot, pos, split, copies, xk2, chunk, 3, lambda: sum01(chunk))

            with dve.Fori(0, GROUPS - 1) as bt:
                group(bt, False)
            group(GROUPS - 1, True)
            sum2(GROUPS * CHUNKS)

        @block.scalar
        def _(act):
            def fill_stage(bt):
                if not (isinstance(bt, int) and bt == 0):
                    act.wait_ge(xt_stored, 16 * ST_DMAS * bt)
                for q in range(2):
                    act.wait_ge(turned_ready, 2 * bt + q + 1)
                    nc.scalar.copy(stage[0:2 * F, :, 4 * q:4 * q + 4, :].rearrange("p c d b -> p d c b"),
                                   turned[q][0:2 * F].rearrange("p (d c b) -> p d c b", d=4, c=CHUNKS)
                                   ).then_inc(stage_ready, 1)

            def round_slots(slots, slot, pos, split):
                for k in slots:
                    act.wait_ge(prod_ready, slot + k + 1)
                    held = prod[:, (pos + k) % RING]
                    if k == HALF_SLOT:
                        nc.scalar.copy(half_parts[:], held[:, 1, :]).then_inc(hi_ready, 1)
                    else:
                        nc.scalar.copy(prod_hi[:, split % SPLIT_RING], held).then_inc(hi_ready, 1)
                        split += 1
                return split

            def hand_on(layer, xk, b, slots):
                act.wait_ge(slot_free, RING + slots)
                nc.scalar.activation(xk[0:HALF], z[layer][0:HALF], ACT.Relu, bias=b[0:HALF])
                nc.scalar.activation(xk[HALF:P], z[layer][0:HALF], ACT.Relu, bias=b[0:HALF]
                                     ).then_inc(xk_ready[layer], 1)

            def direct_0():
                nc.scalar.activation(direct01[HALF:P], z[0][HALF:P], ACT.Relu, bias=b0_sb[HALF:P]
                                     ).then_inc(direct01_ready, 1)

            def direct_2(chunk, slots):
                act.wait_ge(slot_free, RING + slots)
                act.wait_ge(summed2, chunk + 1)
                nc.scalar.activation(direct2[:], z[2][:], ACT.Relu, bias=b2_sb[:]
                                     ).then_inc(direct2_ready, 1)

            act.wait_ge(raw_in, 16 * RAW_DMAS)
            for n in range(2):
                nc.scalar.copy(w_hi[n][:].rearrange("p t s -> p (t s)"), w_raw[n]
                               ).then_inc(w_hi_ready, 1)
            act.wait_ge(weights_in, 16 * WEIGHT_DMAS)
            fill_stage(0)
            hand_on(0, xk1, b0_sb, SL0)
            direct_0()

            def group(bt, last):
                split = 0
                for c in range(CHUNKS):
                    chunk = bt * CHUNKS + c
                    slot, pos = SL0 + chunk * SLC, SL0 + c * SLC
                    split = round_slots(ROUNDED_SLOTS[:EARLY], slot, pos, split)
                    direct_2(chunk, slot)
                    split = round_slots(ROUNDED_SLOTS[EARLY:], slot, pos, split)
                    slot, pos = slot + SLX, pos + SLX
                    hand_on(1, xk2, b1_sb, slot)
                    nc.scalar.activation(direct01[0:HALF], z[1][HALF:P], ACT.Relu, bias=b1_sb[HALF:P]
                                         ).then_inc(direct01_ready, 1)
                    if c == 1 and not last:
                        fill_stage(bt + 1)
                    if last and c == CHUNKS - 1:
                        split = round_slots(ROUNDED_SLOTS, slot, pos, split)
                    else:
                        slot, pos = slot + SL0, pos + SL0
                        split = round_slots(ROUNDED_SLOTS[:EARLY], slot, pos, split)
                        hand_on(0, xk1, b0_sb, slot)
                        act.wait_ge(summed01, chunk + 1)
                        direct_0()
                        split = round_slots(ROUNDED_SLOTS[EARLY:], slot, pos, split)

            with act.Fori(0, GROUPS - 1) as bt:
                group(bt, False)
            group(GROUPS - 1, True)
            direct_2(GROUPS * CHUNKS, SLC * CHUNKS * GROUPS)

            for step, (kind, n, m) in enumerate(TOP_ORDER):
                act.wait_ge(h_ready, step + 1)
                acc = top[step % len(top)]
                if kind == "h1":
                    nc.scalar.activation(h1_sb[:, n % 2, m, :], acc[:], ACT.Relu,
                                         bias=bt1_sb[:, m:m + 1]).then_inc(h_relu, 1)
                elif kind == "h2":
                    nc.scalar.activation(h2_sb[:, n % 2, m, :], acc[:], ACT.Relu,
                                         bias=bt2_sb[:, m:m + 1]).then_inc(h_relu, 1)
                else:
                    nc.scalar.copy(y_sb[:, n * NB:(n + 1) * NB], acc[0:1, :]).then_inc(h_relu, 1)

        @block.tensor
        def _(pe):
            def transpose_group(bt):
                pe.wait_ge(gathered, 16 * F * (bt + 1))
                if not (isinstance(bt, int) and bt == 0):
                    pe.wait_ge(stage_ready, 2 * bt)
                for d in range(D // 2):
                    ins = nc.tensor.transpose(turned[d // 4][0:2 * F, d % 4 * P:(d % 4 + 1) * P],
                                              emb[:, d:F * D:D // 2], ident[:])
                    if d % 4 == 3:
                        ins.then_inc(turned_ready, 1)

            def layer0(slot, pos):
                for k in range(SL0):
                    pe.wait_ge(prod_ready, slot + k + 1)
                    for t in range(2 * k, min(2 * k + 2, T0)):
                        rows = R0_LAST if t == T0 - 1 else R0
                        ins = nc.tensor.matmul(z[0][:], w0_sb[0:rows, t, :],
                                               prod[0:rows, (pos + k) % RING, t % 2, :],
                                               start=(t == 0), stop=(t == T0 - 1))
                    ins.then_inc(slot_free, 1)

            def layer(n, slot, pos, split, chunk):
                whole, hi, lo = w_plain[n - 1], w_hi[n - 1], w_lo[n - 1]
                for k in range(SLX):
                    held = prod[:, (pos + k) % RING]
                    if k in ROUNDED_SLOTS:
                        pe.wait_ge(lo_ready, (chunk * 2 + n - 1) * ROUNDED + ROUNDED_SLOTS.index(k) + 1)
                    else:
                        pe.wait_ge(prod_ready, slot + k + 1)
                    terms = []
                    for place, t in enumerate(SLOT_TILES[k]):
                        if t == TX - 1:
                            i = SPLITS - 1
                            terms += [(lo[:, i, :], half_parts[:]), (hi[:, i, :], half_parts[:])]
                        elif t in SPLIT_TILES:
                            i = SPLIT_TILES.index(t)
                            p_hi = prod_hi[:, split % SPLIT_RING, place, :]
                            p_lo = prod_lo[:, split % SPLIT_RING, place, :]
                            terms += [(lo[:, i, :], p_hi), (hi[:, i, :], p_lo), (hi[:, i, :], p_hi)]
                        else:
                            terms.append((whole[:, PLAIN_TILES.index(t), :], held[:, place, :]))
                    for i, (w, x) in enumerate(terms):
                        ins = nc.tensor.matmul(z[n][:], w, x, start=(k == i == 0),
                                               stop=(k == SLX - 1 and i == len(terms) - 1))
                    ins.then_inc(slot_free, 1)
                    split += k in SPLIT_SLOTS
                return split

            pe.wait_ge(ident_ready, 1)
            transpose_group(0)
            pe.wait_ge(w0_summed, 1)
            pe.wait_ge(w_split, 2)
            pe.wait_ge(weights_in, 16 * WEIGHT_DMAS)
            layer0(0, 0)

            def group(bt, last):
                split = 0
                for c in range(CHUNKS):
                    chunk = bt * CHUNKS + c
                    slot, pos = SL0 + chunk * SLC, SL0 + c * SLC
                    pe.wait_ge(direct01_ready, 2 * chunk + 1)
                    split = layer(1, slot, pos, split, chunk)
                    slot, pos = slot + SLX, pos + SLX
                    if c == 1 and not last:
                        transpose_group(bt + 1)
                    if not (last and c == CHUNKS - 1):
                        layer0(slot, pos)
                        slot, pos = slot + SL0, pos + SL0
                    pe.wait_ge(direct2_ready, chunk + 1)
                    split = layer(2, slot, pos, split, chunk)

            with pe.Fori(0, GROUPS - 1) as bt:
                group(bt, False)
            group(GROUPS - 1, True)

            pe.wait_ge(top_weights_in, 16 * TOP_DMAS)
            pe.wait_ge(summed01, GROUPS * CHUNKS)
            pe.wait_ge(summed2, GROUPS * CHUNKS + 2)
            pe.wait_ge(direct2_ready, GROUPS * CHUNKS + 1)
            for step, (kind, n, m) in enumerate(TOP_ORDER):
                acc = top[step % len(top)]
                if step >= len(top):
                    pe.wait_ge(h_relu, step - len(top) + 1)
                cols, rows = slice(n * NB, (n + 1) * NB), slice(m * P, (m + 1) * P)
                if kind == "h1":
                    terms = [(wt1a_sb[:, rows], logit01[:, cols]),
                             (wt1b_sb[:, rows], logit2[:, CB + n * NB:CB + (n + 1) * NB]),
                             (wt1c_sb[:, rows], dense_sb[:, cols])]
                elif kind == "h2":
                    pe.wait_ge(h_relu, last_h1(n))
                    terms = [(wt2_sb[:, k, rows], h1_sb[:, n % 2, k, :]) for k in range(H1 // P)]
                else:
                    pe.wait_ge(h_relu, step)
                    terms = [(wt3_sb[:, k:k + 1], h2_sb[:, n % 2, k, :]) for k in range(H2 // P)]
                for k, (w, x) in enumerate(terms):
                    ins = nc.tensor.matmul(acc[0:w.shape[1]], w, x, start=(k == 0),
                                           stop=(k == len(terms) - 1))
                ins.then_inc(h_ready, 1)


def kernel(**inputs):
    import numpy as np
    import concourse.bacc as bacc
    from concourse.bass_utils import run_bass_kernel_spmd

    raw = {k: np.asarray(v) for k, v in inputs.items()}
    h = np.arange(F)
    w0 = raw["L0_rec_w0"]
    w0f = np.zeros((R0, T0, S), w0.dtype)
    w0s = np.zeros((R0, T0, S), w0.dtype)
    for j in range(F // 2 + 1):
        t, rows = j // DIAG, slice(j % DIAG * F, (j % DIAG + 1) * F)
        w0f[rows, t] = w0[h, (h + j) % F]
        if j > 0:
            w0s[rows, t] = w0[(h + j) % F, h]

    def by_tile(w):
        rows = w.reshape(F * HALF, S)
        tiles = [rows[t * P:(t + 1) * P] for t in PLAIN_TILES + SPLIT_TILES]
        tiles.append(np.concatenate([rows[(TX - 1) * P:]] * 2))
        return np.ascontiguousarray(np.stack(tiles, axis=1))

    arrays = {f"in_tbl_{f}": raw[f"tbl_{f}"] for f in range(F)}
    arrays.update(
        in_ids=raw["ids"],
        in_dense_t=np.ascontiguousarray(raw["dense_ctx"].T),
        in_w0f=w0f.reshape(R0, T0 * S),
        in_w0s=w0s.reshape(R0, T0 * S),
        in_w1=by_tile(raw["L0_rec_w1"]),
        in_w2=by_tile(raw["L0_rec_w2"]),
        in_b0=raw["L0_rec_b0"].reshape(S, 1),
        in_b1=raw["L0_rec_b1"].reshape(S, 1),
        in_b2=raw["L0_rec_b2"].reshape(S, 1),
        in_wt1=raw["W_top1"],
        in_bt1=np.ascontiguousarray(raw["b_top1"].reshape(H1 // P, P).T),
        in_wt2=raw["W_top2"],
        in_bt2=np.ascontiguousarray(raw["b_top2"].reshape(H2 // P, P).T),
        in_wt3=np.ascontiguousarray(raw["W_top3"].reshape(H2 // P, P).T),
    )
    nc = bacc.Bacc("TRN2", target_bir_lowering=False, num_devices=1)
    aps = {k: nc.dram_tensor(k, a.shape, mybir.dt.from_np(a.dtype), kind="ExternalInput").ap()
           for k, a in arrays.items()}
    out = nc.dram_tensor("out_y", (1, B), F32, kind="ExternalOutput").ap()
    names = ["ids", "dense_t", "w0f", "w0s", "w1", "w2", "b0", "b1", "b2",
             "wt1", "bt1", "wt2", "bt2", "wt3"]
    build(nc, [aps[f"in_tbl_{f}"] for f in range(F)], *(aps["in_" + k] for k in names), out)
    r = run_bass_kernel_spmd(nc, [arrays], core_ids=[0])
    return r.results[0]["out_y"].reshape(B, 1)
```

```python
import concourse.bass as bass
from concourse import mybir
from contextlib import ExitStack

F32 = mybir.dt.float32
I32 = mybir.dt.int32
F32R = mybir.dt.float32r
ALU = mybir.AluOpType
ACT = mybir.ActivationFunctionType
AXIS = mybir.AxisListType

B, F, D, P = 2048, 39, 16, 128
S = 128
HALF = S // 2
GROUPS = B // P
CHUNKS = 4
CB = P // CHUNKS
N = CB * D
DIAG = 3
T0 = 7
R0 = DIAG * F
R0_LAST = 2 * F
TX = 20
WRAP = 20
COLS = B * D
QUAD = 4
RING = 4
SL0, SLX = -(-T0 // QUAD), TX // QUAD
SLC = SL0 + 2 * SLX
FIRST_TILE = (0, 4, 16, 8, 12)
SPLITS0 = [(0, 0, 2)]
SPLITSX = [(1, 0, 2), (2, 0, 2), (2, 3, 1), (3, 0, 2)]
EARLY = 3
SPLITS_C = len(SPLITS0) + 2 * len(SPLITSX)
PAIR_RING = 2
assert GROUPS and CHUNKS * sum(n == 2 for _, _, n in SPLITS0 + 2 * SPLITSX) % PAIR_RING == 0
SPLIT_TILES = [FIRST_TILE[k] + at + i for k, at, n in SPLITSX for i in range(n) if n == 2]
PLAIN_TILES = [t for t in range(TX - 1) if t not in SPLIT_TILES]
W_SPLITS = len(SPLIT_TILES) + 1
W_ORDER = (1, 2, 0)
X0_DIAG_DMAS, X0_PAIRS_DMAS, ST_DMAS = 2 * DIAG, 3, 4
RAW_DMAS, WEIGHT_DMAS, TOP_DMAS = 4, 8, 6
H1, H2, DENSE = 512, 256, 16
NB = 512


def top_order():
    steps = []
    for n in range(B // NB + 1):
        if n < B // NB:
            steps += [("h1", n, m) for m in range(H1 // P)]
        if n > 0:
            steps += [("h2", n - 1, m) for m in range(H2 // P)] + [("y", n - 1, 0)]
    return steps


TOP_ORDER = top_order()
TOP_STEPS = len(TOP_ORDER)


def last_h1(n):
    return TOP_ORDER.index(("h1", n, H1 // P - 1)) + 1


def build(nc, tables, ids, dense_t, w0f, w0s, w1, w2, b0, b1, b2, wt1, bt1, wt2, bt2, wt3, out):
    xt = nc.dram_tensor("x0_transposed", [F + WRAP, COLS], F32, kind="Internal").ap()

    ctx = ExitStack()
    with ctx:
        def sb(name, shape, dt=F32):
            return ctx.enter_context(nc.sbuf_tensor(name, shape, dt))

        def ps(name):
            return ctx.enter_context(nc.psum_tensor(name, [P, N], F32))

        def sem(name):
            return ctx.enter_context(nc.semaphore(name))

        x0_pairs = [sb(f"x0_pairs{i}", [P, TX, N]) for i in range(2)]
        x0_diag = sb("x0_diag", [P, T0 + 1, N])
        prod = sb("prod", [P, RING, QUAD, N])
        pair_hi = sb("pair_hi", [P, PAIR_RING, 2, N], F32R)
        pair_lo = sb("pair_lo", [P, PAIR_RING, 2, N], F32R)
        half_parts = sb("half_parts", [P, N], F32R)
        xk1 = sb("xk1", [P, N])
        xk2 = sb("xk2", [P, N])
        logit01 = sb("logit01", [P, CB + B])
        logit2 = sb("logit2", [P, CB + B])
        idx = sb("idx", [P, F], I32)
        emb = sb("emb", [P, F * D])
        stage = sb("stage", [P, CHUNKS, D // 2, CB])
        ident = sb("ident", [P, P])
        w0_sb = sb("w0_sb", [P, T0, S])
        w_plain = [sb(f"w{n}_plain", [P, len(PLAIN_TILES), S]) for n in (1, 2)]
        splits = [2, W_SPLITS, W_SPLITS]
        w_hi = [sb(f"w{n}_hi", [P, splits[n], S], F32R) for n in range(3)]
        w_lo = [sb(f"w{n}_lo", [P, splits[n], S], F32R) for n in range(3)]
        wt3_sb = sb("wt3_sb", [P, H2 // P])
        b0_sb = sb("b0_sb", [P, 1])
        b1_sb = sb("b1_sb", [P, 1])
        b2_sb = sb("b2_sb", [P, 1])
        bt1_sb = sb("bt1_sb", [P, H1 // P])
        bt2_sb = sb("bt2_sb", [P, H2 // P])
        w0_swapped = x0_pairs[1][0:R0, 0:2, :].rearrange("p a n -> p (a n)")[:, 0:T0 * S]
        w_raw = [x0_pairs[1][:, 2 + 2 * i:4 + 2 * i, :].rearrange("p a n -> p (a n)")[:, 0:W_SPLITS * S]
                 for i in range(2)]
        w_raw.insert(0, w0_sb[0:R0, 0:2, :].rearrange("p t s -> p (t s)"))
        def top_part(first, n):
            return x0_pairs[0][:, first:first + n, :].rearrange("p a n -> p (a n)")

        wt1a_sb, wt1b_sb, wt1c_sb = top_part(0, 1), top_part(1, 1), top_part(2, 1)[0:DENSE]
        wt2_sb = top_part(3, 2).rearrange("p (t n) -> p t n", n=H2)
        dense_sb = top_part(5, 4)[0:DENSE]
        h2_sb = top_part(9, 4).rearrange("p (i m n) -> p i m n", i=2, n=NB)
        y_sb = top_part(13, 4)[0:1]
        h1_sb = x0_diag[:].rearrange("p (i m) n -> p i m n", i=2)

        z = [ps("z0"), ps("z1"), ps("z2")]
        turned = [ps("turned0"), ps("turned1")]
        direct01 = [ps("direct01_0"), ps("direct01_1")]
        direct2 = ps("direct2")
        top = z + direct01 + [direct2]

        swapped_in = sem("swapped_in")
        raw_in = sem("raw_in")
        w0_summed = sem("w0_summed")
        w_hi_ready = sem("w_hi_ready")
        w_split = sem("w_split")
        weights_in = sem("weights_in")
        top_weights_in = sem("top_weights_in")
        ident_zero = sem("ident_zero")
        ident_ready = sem("ident_ready")
        idx_in = sem("idx_in")
        gather_started = sem("gather_started")
        gathered = sem("gathered")
        turned_ready = sem("turned_ready")
        stage_ready = sem("stage_ready")
        xt_stored = sem("xt_stored")
        x0_diag_in = sem("x0_diag_in")
        x0_pairs_in = [sem(f"x0_pairs_in{i}") for i in range(2)]
        prod_ready = sem("prod_ready")
        hi_ready = sem("hi_ready")
        lo_ready = sem("lo_ready")
        slot_free = sem("slot_free")
        xk_ready = [sem("xk1_ready"), sem("xk2_ready")]
        direct01_ready = sem("direct01_ready")
        direct2_ready = sem("direct2_ready")
        direct01_cleared = sem("direct01_cleared")
        summed01 = sem("summed01")
        summed2 = sem("summed2")
        h_ready = sem("h_ready")
        h_relu = sem("h_relu")
        y_stored = sem("y_stored")

        block = ctx.enter_context(nc.Block())

        @block.sync
        def _(sp):
            sp.dma_start(w0_swapped, w0s).then_inc(swapped_in, 16)
            sp.dma_start(w0_sb[0:R0].rearrange("p t s -> p (t s)"), w0f).then_inc(swapped_in, 16)
            plain = len(PLAIN_TILES)
            for n, w in enumerate((w1, w2)):
                raw = w_raw[n + 1].rearrange("p (t s) -> p t s", s=S)
                sp.dma_start(raw[:, 0:W_SPLITS - 1], w[:, plain:TX - 1]).then_inc(raw_in, 16)
                sp.dma_start(raw[:, W_SPLITS - 1], w[:, TX - 1]).then_inc(raw_in, 16)
            loads = [(w_plain[0][:], w1[:, 0:plain]), (w_plain[1][:], w2[:, 0:plain]),
                     (b0_sb[:], b0), (b1_sb[:], b1), (b2_sb[:], b2),
                     (bt1_sb[:], bt1), (bt2_sb[:], bt2), (wt3_sb[:], wt3)]
            assert len(loads) == WEIGHT_DMAS
            for dst, src in loads:
                sp.dma_start(dst, src).then_inc(weights_in, 16)

            slots_done = sp.alloc_register("slots_done")

            def ahead(value):
                return value if isinstance(value, int) else sp.snap(value)

            def store_group(bt):
                first = ahead(bt * (P * D))
                sp.wait_ge(stage_ready, 2 * (bt + 1))
                cols = xt[:, bass.ds(first, P * D)].rearrange(
                    "f (c e n) -> f c e n", c=CHUNKS, e=2)
                for half in range(2):
                    src = stage[half:2 * F:2].rearrange("p c d b -> p c (d b)")
                    sp.dma_start(cols[0:F, :, half, :], src).then_inc(xt_stored, 16)
                    sp.dma_start(cols[F:F + WRAP, :, half, :], src[0:WRAP]).then_inc(xt_stored, 16)

            def load_chunk(bt, c):
                first = ahead(bt * (P * D) + c * N)
                slots = (bt * CHUNKS + c) * SLC - SLC + SL0 + 1
                if not isinstance(bt, int):
                    sp.reg_mov(slots_done, slots)
                    slots = slots_done
                if c == 0:
                    sp.wait_ge(xt_stored, 16 * ST_DMAS * (bt + 1))
                if not (isinstance(bt, int) and bt == c == 0):
                    sp.wait_ge(prod_ready, slots)
                chunk = xt[:, bass.ds(first, N)]
                for i in range(DIAG):
                    rows = slice(i * F, (i + 1) * F)
                    shifted = bass.AP(tensor=chunk.tensor, offset=chunk[i:i + F].offset,
                                      ap=[[COLS, F], [DIAG * COLS, T0], [1, N]])
                    sp.dma_start(x0_diag[rows, 0:T0, :], shifted).then_inc(x0_diag_in, 16)
                    sp.dma_start(x0_diag[rows, T0, :], chunk[0:F]).then_inc(x0_diag_in, 16)
                buf, loaded = x0_pairs[c % 2], x0_pairs_in[c % 2]
                for half in range(2):
                    src = chunk[half:half + F - 1].rearrange("(t two) n -> t two n", two=2)[:, 0, :]
                    sp.dma_start(buf[half * HALF:(half + 1) * HALF, 0:TX - 1, :],
                                 src.partition_broadcast(HALF)).then_inc(loaded, 16)
                src = chunk[F - 1:F].rearrange("o n -> (o n)")
                sp.dma_start(buf[:, TX - 1, :], src.partition_broadcast(P)).then_inc(loaded, 16)

            def load_top():
                sp.wait_ge(prod_ready, (GROUPS * CHUNKS - 1) * SLC + SL0 + 1)
                loads = [
                    (wt1a_sb[0:HALF], wt1[HALF:P]), (wt1a_sb[HALF:P], wt1[0:HALF]),
                    (wt1b_sb, wt1[P:2 * P]), (wt1c_sb, wt1[2 * P:2 * P + DENSE]),
                    (wt2_sb, wt2.rearrange("(t p) n -> p t n", p=P)), (dense_sb, dense_t),
                ]
                assert len(loads) == TOP_DMAS
                for dst, src in loads:
                    sp.dma_start(dst, src).then_inc(top_weights_in, 16)

            store_group(0)
            sp.wait_ge(w0_summed, 1)
            sp.wait_ge(w_split, 3)
            load_chunk(0, 0)

            def group(bt, last):
                for c in range(CHUNKS):
                    if c == 2 and not last:
                        store_group(bt + 1)
                    if c < CHUNKS - 1:
                        load_chunk(bt, c + 1)
                    elif not last:
                        load_chunk(bt + 1, 0)
                    else:
                        load_top()

            with sp.Fori(0, GROUPS - 1) as bt:
                group(bt, False)
            group(GROUPS - 1, True)
            sp.wait_ge(h_relu, TOP_STEPS)
            sp.dma_start(out, y_sb).then_inc(y_stored, 16)
            sp.wait_ge(y_stored, 16)

        @block.gpsimd
        def _(pool):
            nc.gpsimd.memset(ident[:], 0.0).then_inc(ident_zero, 1)
            pool.wait_ge(ident_zero, 1)
            nc.gpsimd.affine_select(out=ident[:], in_=ident[:], compare_op=ALU.not_equal, fill=1.0,
                                    base=0, pattern=[[-1, P]], channel_multiplier=1
                                    ).then_inc(ident_ready, 1)

            def gather(bt, first):
                if not first:
                    pool.wait_ge(gathered, 16 * F * bt)
                    pool.sem_inc(gather_started, 1)
                pool.dma_start(idx[:], ids[bass.ds(bt * P, P), :]).then_inc(idx_in, 16)
                pool.wait_ge(idx_in, 16 * (bt + 1))
                if not first:
                    pool.wait_ge(turned_ready, 2 * bt)
                pool.sem_inc(gather_started, 1)
                for f in range(F):
                    nc.gpsimd.indirect_dma_start(
                        out=emb[:, f * D:(f + 1) * D], out_offset=None, in_=tables[f],
                        in_offset=bass.IndirectOffsetOnAxis(ap=idx[:, f:f + 1], axis=0),
                    ).then_inc(gathered, 16)

            gather(0, True)
            with pool.Fori(1, GROUPS) as bt:
                gather(bt, False)

        @block.vector
        def _(dve):
            nc.vector.memset(direct01[1][:], 0.0).then_inc(direct01_cleared, 1)
            nc.vector.memset(z[2][:], 0.0).then_inc(summed2, 1)
            dve.sem_inc(slot_free, RING)
            dve.wait_ge(swapped_in, 32)
            w0 = w0_sb[0:R0].rearrange("p t s -> p (t s)")
            nc.vector.tensor_tensor(w0, w0, w0_swapped, ALU.add).then_inc(w0_summed, 1)
            for i, n in enumerate(W_ORDER):
                rows = w_raw[n].shape[0]
                dve.wait_ge(w_hi_ready, i + 1)
                nc.vector.tensor_tensor(w_lo[n][0:rows].rearrange("p t s -> p (t s)"), w_raw[n],
                                        w_hi[n][0:rows].bitcast(F32).rearrange("p t s -> p (t s)"),
                                        ALU.subtract).then_inc(w_split, 1)

            def product(slot, pos, a, xk):
                rows, n = a.shape[0], a.shape[1]
                dve.wait_ge(slot_free, slot + 1)
                nc.vector.tensor_tensor(prod[0:rows, pos % RING, 0:n, :], a,
                                        xk.unsqueeze(1).broadcast_to([rows, n, N]),
                                        ALU.mult).then_inc(prod_ready, 1)

            def low_parts(split, rows, pos, at, n, pair):
                dve.wait_ge(hi_ready, split + 1)
                held = prod[:, pos % RING]
                if n == 1:
                    nc.vector.tensor_tensor(half_parts[HALF:P], held[HALF:P, at, :],
                                            half_parts[HALF:P].bitcast(F32),
                                            ALU.subtract).then_inc(lo_ready, 1)
                else:
                    nc.vector.tensor_tensor(pair_lo[0:rows, pair % PAIR_RING],
                                            held[0:rows, at:at + 2, :],
                                            pair_hi[0:rows, pair % PAIR_RING].bitcast(F32),
                                            ALU.subtract).then_inc(lo_ready, 1)

            def layer(splits, first_tile, tiles, rows, copies, xk, slot, pos, split, pair):
                for k, t in enumerate(first_tile):
                    product(slot + k, pos + k, copies[0:rows, t:min(t + QUAD, tiles), :], xk)
                    for at_slot, at, n in splits:
                        if at_slot == k - 1:
                            low_parts(split, rows, pos + at_slot, at, n, pair)
                            split = split + 1
                            pair += n == 2
                return split, pair

            def layer0(slot, pos, chunk, split, pair):
                dve.wait_ge(x0_diag_in, 16 * X0_DIAG_DMAS * (chunk + 1))
                return layer(SPLITS0, range(0, T0, QUAD), T0, R0, x0_diag, x0_diag[0:R0, T0, :],
                             slot, pos, split, pair)

            def sum01(chunk, c):
                nc.vector.tensor_reduce(logit01[:, bass.ds(chunk * CB, CB)],
                                        direct01[(c - 1) % 2][:].rearrange("p (d b) -> p b d", b=CB),
                                        AXIS.X, ALU.add).then_inc(summed01, 1)

            def sum2(chunk):
                dve.wait_ge(direct2_ready, chunk + 1)
                nc.vector.tensor_reduce(logit2[:, bass.ds(chunk * CB, CB)],
                                        direct2[:].rearrange("p (d b) -> p b d", b=CB),
                                        AXIS.X, ALU.add).then_inc(summed2, 1)

            dve.wait_ge(direct01_cleared, 1)
            layer0(0, 0, 0, 0, 0)

            def group(bt, last):
                pair = 1
                for c in range(CHUNKS):
                    chunk = bt * CHUNKS + c
                    slot, pos = SL0 + chunk * SLC, SL0 + c * SLC
                    split = len(SPLITS0) + chunk * SPLITS_C
                    copies = x0_pairs[c % 2]
                    dve.wait_ge(x0_pairs_in[c % 2],
                                16 * X0_PAIRS_DMAS * (bt * (CHUNKS // 2) + c // 2 + 1))
                    dve.wait_ge(xk_ready[0], chunk + 1)
                    split, pair = layer(SPLITSX, FIRST_TILE, TX, P, copies, xk1[:],
                                        slot, pos, split, pair)
                    slot, pos = slot + SLX, pos + SLX
                    if not (last and c == CHUNKS - 1):
                        split, pair = layer0(slot, pos, chunk + 1, split, pair)
                        slot, pos = slot + SL0, pos + SL0
                    sum2(chunk)
                    dve.wait_ge(direct01_ready, 2 * chunk + 1)
                    sum01(chunk, c)
                    dve.wait_ge(xk_ready[1], chunk + 1)
                    split, pair = layer(SPLITSX, FIRST_TILE, TX, P, copies, xk2[:],
                                        slot, pos, split, pair)

            with dve.Fori(0, GROUPS - 1) as bt:
                group(bt, False)
            group(GROUPS - 1, True)
            dve.wait_ge(direct01_ready, 2 * GROUPS * CHUNKS)
            sum01(GROUPS * CHUNKS, 0)
            sum2(GROUPS * CHUNKS)

        @block.scalar
        def _(act):
            def fill_stage(bt):
                if not (isinstance(bt, int) and bt == 0):
                    act.wait_ge(xt_stored, 16 * ST_DMAS * bt)
                for q in range(2):
                    act.wait_ge(turned_ready, 2 * bt + q + 1)
                    nc.scalar.copy(stage[0:2 * F, :, 4 * q:4 * q + 4, :].rearrange("p c d b -> p d c b"),
                                   turned[q][0:2 * F].rearrange("p (d c b) -> p d c b", d=4, c=CHUNKS)
                                   ).then_inc(stage_ready, 1)

            def round_splits(splits, rows, slot, pos, pair, held_by):
                for k, at, n in splits:
                    act.wait_ge(prod_ready, slot + k + 1)
                    held = prod[0:rows, (pos + k) % RING]
                    if n == 1:
                        nc.scalar.copy(half_parts[:], held[:, at, :]).then_inc(hi_ready, 1)
                    else:
                        act.wait_ge(slot_free, RING + held_by[-PAIR_RING] + 1)
                        nc.scalar.copy(pair_hi[0:rows, pair % PAIR_RING], held[:, at:at + 2, :]
                                       ).then_inc(hi_ready, 1)
                        held_by.append(slot + k)
                        pair += 1
                return pair

            def hand_on(layer, xk, b, slots):
                act.wait_ge(slot_free, RING + slots)
                nc.scalar.activation(xk[0:HALF], z[layer][0:HALF], ACT.Relu, bias=b[0:HALF])
                nc.scalar.activation(xk[HALF:P], z[layer][0:HALF], ACT.Relu, bias=b[0:HALF]
                                     ).then_inc(xk_ready[layer], 1)

            def direct_0(c):
                nc.scalar.activation(direct01[c % 2][HALF:P], z[0][HALF:P], ACT.Relu, bias=b0_sb[HALF:P]
                                     ).then_inc(direct01_ready, 1)

            def direct_2(chunk, slots):
                act.wait_ge(slot_free, RING + slots)
                act.wait_ge(summed2, chunk + 1)
                nc.scalar.activation(direct2[:], z[2][:], ACT.Relu, bias=b2_sb[:]
                                     ).then_inc(direct2_ready, 1)

            act.wait_ge(raw_in, 16 * RAW_DMAS)
            for n in W_ORDER:
                if n == 0:
                    act.wait_ge(w0_summed, 1)
                nc.scalar.copy(w_hi[n][0:w_raw[n].shape[0]].rearrange("p t s -> p (t s)"), w_raw[n]
                               ).then_inc(w_hi_ready, 1)
            act.wait_ge(weights_in, 16 * WEIGHT_DMAS)
            fill_stage(0)
            act.wait_ge(prod_ready, 1)
            nc.scalar.copy(pair_hi[0:R0, 0], prod[0:R0, 0, 0:2, :]).then_inc(hi_ready, 1)
            hand_on(0, xk1, b0_sb, SL0)
            direct_0(0)

            def group(bt, last):
                pair = 1
                before = SL0 + bt * CHUNKS * SLC
                held_by = [before - 3, before - 2]
                for c in range(CHUNKS):
                    chunk = bt * CHUNKS + c
                    slot, pos = SL0 + chunk * SLC, SL0 + c * SLC
                    pair = round_splits(SPLITSX[:EARLY], P, slot, pos, pair, held_by)
                    direct_2(chunk, slot)
                    pair = round_splits(SPLITSX[EARLY:], P, slot, pos, pair, held_by)
                    slot, pos = slot + SLX, pos + SLX
                    if not (last and c == CHUNKS - 1):
                        pair = round_splits(SPLITS0, R0, slot, pos, pair, held_by)
                    hand_on(1, xk2, b1_sb, slot)
                    nc.scalar.activation(direct01[c % 2][0:HALF], z[1][HALF:P], ACT.Relu, bias=b1_sb[HALF:P]
                                         ).then_inc(direct01_ready, 1)
                    if c == 1 and not last:
                        fill_stage(bt + 1)
                    if last and c == CHUNKS - 1:
                        round_splits(SPLITSX, P, slot, pos, pair, held_by)
                    else:
                        slot, pos = slot + SL0, pos + SL0
                        pair = round_splits(SPLITSX[:EARLY], P, slot, pos, pair, held_by)
                        hand_on(0, xk1, b0_sb, slot)
                        act.wait_ge(summed01, chunk + 1)
                        direct_0(c + 1)
                        pair = round_splits(SPLITSX[EARLY:], P, slot, pos, pair, held_by)

            with act.Fori(0, GROUPS - 1) as bt:
                group(bt, False)
            group(GROUPS - 1, True)
            direct_2(GROUPS * CHUNKS, SLC * CHUNKS * GROUPS)

            for step, (kind, n, m) in enumerate(TOP_ORDER):
                act.wait_ge(h_ready, step + 1)
                acc = top[step % len(top)]
                if kind == "h1":
                    nc.scalar.activation(h1_sb[:, n % 2, m, :], acc[:], ACT.Relu,
                                         bias=bt1_sb[:, m:m + 1]).then_inc(h_relu, 1)
                elif kind == "h2":
                    nc.scalar.activation(h2_sb[:, n % 2, m, :], acc[:], ACT.Relu,
                                         bias=bt2_sb[:, m:m + 1]).then_inc(h_relu, 1)
                else:
                    nc.scalar.copy(y_sb[:, n * NB:(n + 1) * NB], acc[0:1, :]).then_inc(h_relu, 1)

        @block.tensor
        def _(pe):
            def transpose_group(bt):
                pe.wait_ge(gathered, 16 * F * (bt + 1))
                if not (isinstance(bt, int) and bt == 0):
                    pe.wait_ge(stage_ready, 2 * bt)
                for d in range(D // 2):
                    ins = nc.tensor.transpose(turned[d // 4][0:2 * F, d % 4 * P:(d % 4 + 1) * P],
                                              emb[:, d:F * D:D // 2], ident[:])
                    if d % 4 == 3:
                        ins.then_inc(turned_ready, 1)

            def layer(n, splits, first_tile, weights, slot, pos, split, pair):
                whole, hi, lo = weights, w_hi[n], w_lo[n]
                last_slot = len(first_tile) - 1
                for k, t in enumerate(first_tile):
                    held = prod[:, (pos + k) % RING]
                    here = [s for s in splits if s[0] == k]
                    places = range(QUAD if n else min(QUAD, T0 - t))
                    plain = [i for i in places if not any(at <= i < at + m for _, at, m in here)]
                    pe.wait_ge(prod_ready, slot + k + 1)
                    for i in plain:
                        if n:
                            rows, w = P, whole[:, PLAIN_TILES.index(t + i), :]
                        else:
                            rows = R0_LAST if t + i == T0 - 1 else R0
                            w = whole[0:rows, t + i, :]
                        ins = nc.tensor.matmul(z[n][:], w, held[0:rows, i, :],
                                               start=(k == 0 and i == plain[0]),
                                               stop=(k == last_slot and not here and i == plain[-1]))
                    for s in here:
                        _, at, m = s
                        pe.wait_ge(lo_ready, split + 1)
                        if m == 1:
                            terms = [(lo[:, W_SPLITS - 1, :], half_parts[:]),
                                     (hi[:, W_SPLITS - 1, :], half_parts[:])]
                        else:
                            terms = []
                            for i in range(2):
                                j = SPLIT_TILES.index(t + at + i) if n else t + at + i
                                rows = P if n else R0
                                p_hi = pair_hi[0:rows, pair % PAIR_RING, i, :]
                                p_lo = pair_lo[0:rows, pair % PAIR_RING, i, :]
                                w_h, w_l = hi[0:rows, j, :], lo[0:rows, j, :]
                                terms += [(w_l, p_hi), (w_h, p_lo), (w_h, p_hi)]
                            pair += 1
                        for i, (w, x) in enumerate(terms):
                            ins = nc.tensor.matmul(z[n][:], w, x, start=False,
                                                   stop=(k == last_slot and s is here[-1]
                                                         and i == len(terms) - 1))
                        split = split + 1
                    ins.then_inc(slot_free, 1)
                return split, pair

            pe.wait_ge(ident_ready, 1)
            transpose_group(0)
            pe.wait_ge(w0_summed, 1)
            pe.wait_ge(w_split, 3)
            pe.wait_ge(weights_in, 16 * WEIGHT_DMAS)
            layer(0, SPLITS0, range(0, T0, QUAD), w0_sb, 0, 0, 0, 0)

            def group(bt, last):
                pair = 1
                for c in range(CHUNKS):
                    chunk = bt * CHUNKS + c
                    slot, pos = SL0 + chunk * SLC, SL0 + c * SLC
                    split = len(SPLITS0) + chunk * SPLITS_C
                    pe.wait_ge(direct01_ready, 2 * chunk + 1)
                    split, pair = layer(1, SPLITSX, FIRST_TILE, w_plain[0], slot, pos, split, pair)
                    slot, pos = slot + SLX, pos + SLX
                    if c == 1 and not last:
                        transpose_group(bt + 1)
                    if not (last and c == CHUNKS - 1):
                        split, pair = layer(0, SPLITS0, range(0, T0, QUAD), w0_sb,
                                            slot, pos, split, pair)
                        slot, pos = slot + SL0, pos + SL0
                    pe.wait_ge(direct2_ready, chunk + 1)
                    split, pair = layer(2, SPLITSX, FIRST_TILE, w_plain[1], slot, pos, split, pair)

            with pe.Fori(0, GROUPS - 1) as bt:
                group(bt, False)
            group(GROUPS - 1, True)

            pe.wait_ge(top_weights_in, 16 * TOP_DMAS)
            pe.wait_ge(summed01, GROUPS * CHUNKS + 1)
            pe.wait_ge(summed2, GROUPS * CHUNKS + 2)
            pe.wait_ge(direct2_ready, GROUPS * CHUNKS + 1)
            for step, (kind, n, m) in enumerate(TOP_ORDER):
                acc = top[step % len(top)]
                if step >= len(top):
                    pe.wait_ge(h_relu, step - len(top) + 1)
                cols, rows = slice(n * NB, (n + 1) * NB), slice(m * P, (m + 1) * P)
                if kind == "h1":
                    terms = [(wt1a_sb[:, rows], logit01[:, CB + n * NB:CB + (n + 1) * NB]),
                             (wt1b_sb[:, rows], logit2[:, CB + n * NB:CB + (n + 1) * NB]),
                             (wt1c_sb[:, rows], dense_sb[:, cols])]
                elif kind == "h2":
                    pe.wait_ge(h_relu, last_h1(n))
                    terms = [(wt2_sb[:, k, rows], h1_sb[:, n % 2, k, :]) for k in range(H1 // P)]
                else:
                    pe.wait_ge(h_relu, step)
                    terms = [(wt3_sb[:, k:k + 1], h2_sb[:, n % 2, k, :]) for k in range(H2 // P)]
                for k, (w, x) in enumerate(terms):
                    ins = nc.tensor.matmul(acc[0:w.shape[1]], w, x, start=(k == 0),
                                           stop=(k == len(terms) - 1))
                ins.then_inc(h_ready, 1)


def kernel(**inputs):
    import numpy as np
    import concourse.bacc as bacc
    from concourse.bass_utils import run_bass_kernel_spmd

    raw = {k: np.asarray(v) for k, v in inputs.items()}
    h = np.arange(F)
    w0 = raw["L0_rec_w0"]
    w0f = np.zeros((R0, T0, S), w0.dtype)
    w0s = np.zeros((R0, T0, S), w0.dtype)
    for j in range(F // 2 + 1):
        t, rows = j // DIAG, slice(j % DIAG * F, (j % DIAG + 1) * F)
        w0f[rows, t] = w0[h, (h + j) % F]
        if j > 0:
            w0s[rows, t] = w0[(h + j) % F, h]

    def by_tile(w):
        rows = w.reshape(F * HALF, S)
        tiles = [rows[t * P:(t + 1) * P] for t in PLAIN_TILES + SPLIT_TILES]
        tiles.append(np.concatenate([rows[(TX - 1) * P:]] * 2))
        return np.ascontiguousarray(np.stack(tiles, axis=1))

    arrays = {f"in_tbl_{f}": raw[f"tbl_{f}"] for f in range(F)}
    arrays.update(
        in_ids=raw["ids"],
        in_dense_t=np.ascontiguousarray(raw["dense_ctx"].T),
        in_w0f=w0f.reshape(R0, T0 * S),
        in_w0s=w0s.reshape(R0, T0 * S),
        in_w1=by_tile(raw["L0_rec_w1"]),
        in_w2=by_tile(raw["L0_rec_w2"]),
        in_b0=raw["L0_rec_b0"].reshape(S, 1),
        in_b1=raw["L0_rec_b1"].reshape(S, 1),
        in_b2=raw["L0_rec_b2"].reshape(S, 1),
        in_wt1=raw["W_top1"],
        in_bt1=np.ascontiguousarray(raw["b_top1"].reshape(H1 // P, P).T),
        in_wt2=raw["W_top2"],
        in_bt2=np.ascontiguousarray(raw["b_top2"].reshape(H2 // P, P).T),
        in_wt3=np.ascontiguousarray(raw["W_top3"].reshape(H2 // P, P).T),
    )
    nc = bacc.Bacc("TRN2", target_bir_lowering=False, num_devices=1)
    aps = {k: nc.dram_tensor(k, a.shape, mybir.dt.from_np(a.dtype), kind="ExternalInput").ap()
           for k, a in arrays.items()}
    out = nc.dram_tensor("out_y", (1, B), F32, kind="ExternalOutput").ap()
    names = ["ids", "dense_t", "w0f", "w0s", "w1", "w2", "b0", "b1", "b2",
             "wt1", "bt1", "wt2", "bt2", "wt3"]
    build(nc, [aps[f"in_tbl_{f}"] for f in range(F)], *(aps["in_" + k] for k in names), out)
    r = run_bass_kernel_spmd(nc, [arrays], core_ids=[0])
    return r.results[0]["out_y"].reshape(B, 1)
```

```python
import concourse.bass as bass
from concourse import mybir
from contextlib import ExitStack

F32 = mybir.dt.float32
I32 = mybir.dt.int32
F32R = mybir.dt.float32r
ALU = mybir.AluOpType
ACT = mybir.ActivationFunctionType
AXIS = mybir.AxisListType

B, F, D, P = 2048, 39, 16, 128
S = 128
HALF = S // 2
GROUPS = B // P
CHUNKS = 4
CB = P // CHUNKS
N = CB * D
DIAG = 3
T0 = 7
R0 = DIAG * F
R0_LAST = 2 * F
TX = 20
WRAP = 20
COLS = B * D
QUAD = 4
RING = 4
SL0, SLX = -(-T0 // QUAD), TX // QUAD
SLC = SL0 + 2 * SLX
L0_FIRST = range(0, T0, QUAD)
FIRST_TILE = (0, 4, 16, 8, 12)
SPLITS = {0: [(0, 0, 2)],
          1: [(0, 0, 2), (1, 0, 2), (2, 0, 2), (2, 3, 1), (3, 0, 2), (4, 0, 2)],
          2: [(0, 0, 2), (1, 0, 2), (2, 0, 2), (2, 3, 1), (3, 0, 2), (4, 0, 2)]}
EARLY = {1: 4, 2: 4}
SPLITS_C = sum(len(SPLITS[n]) for n in SPLITS)
GATHERS_AHEAD = 30
GATHERS_AT = [range(30, F), range(0, 10), range(10, 20), range(20, 30)]
PAIR_RING = 2
PAIRS = {n: sum(m == 2 for _, _, m in SPLITS[n]) for n in SPLITS}
assert CHUNKS * sum(PAIRS.values()) % PAIR_RING == 0
SPLIT_TILES = {n: [(FIRST_TILE if n else L0_FIRST)[k] + at + i
                   for k, at, m in SPLITS[n] for i in range(m) if m == 2] for n in SPLITS}
PLAIN_TILES = {n: [t for t in range(TX - 1 if n else T0) if t not in SPLIT_TILES[n]] for n in SPLITS}
W_ORDER = (1, 2, 0)
W_SPLITS = {n: len(SPLIT_TILES[n]) + (n > 0) for n in SPLITS}
X0_DIAG_DMAS, X0_PAIRS_DMAS, ST_DMAS = 2 * DIAG, 3, 4
RAW_DMAS, WEIGHT_DMAS, TOP_DMAS = 2, 3, 6
H1, H2, DENSE = 512, 256, 16
DENSE_ROWS = 2 * 32 + DENSE
BT2, WT3 = 3 + H1 // P, 3 + (H1 + H2) // P
COLUMNS = WT3 + H2 // P
NB = 512
assert CB < NB < B and len(SPLITS[0]) == 1


def top_order():
    steps = []
    for n in range(B // NB + 1):
        if n < B // NB:
            steps += [("h1", n, m) for m in range(H1 // P)]
        if n > 0:
            steps += [("h2", n - 1, m) for m in range(H2 // P)] + [("y", n - 1, 0)]
    return steps


TOP_ORDER = top_order()
TOP_STEPS = len(TOP_ORDER)


def last_h1(n):
    return TOP_ORDER.index(("h1", n, H1 // P - 1)) + 1


def build(nc, tables, ids, dense_t, w0f, w0s, w1, w2, small, wt1, wt1c, wt2, out):
    xt = nc.dram_tensor("x0_transposed", [F + WRAP, COLS], F32, kind="Internal").ap()

    ctx = ExitStack()
    with ctx:
        def sb(name, shape, dt=F32):
            return ctx.enter_context(nc.sbuf_tensor(name, shape, dt))

        def ps(name):
            return ctx.enter_context(nc.psum_tensor(name, [P, N], F32))

        def sem(name):
            return ctx.enter_context(nc.semaphore(name))

        x0_pairs = [sb(f"x0_pairs{i}", [P, TX, N]) for i in range(2)]
        x0_diag = sb("x0_diag", [P, T0 + 1, N])
        prod = sb("prod", [P, RING, QUAD, N])
        pair_hi = sb("pair_hi", [P, PAIR_RING, 2, N], F32R)
        pair_lo = sb("pair_lo", [P, PAIR_RING, 2, N], F32R)
        half_parts = sb("half_parts", [P, N], F32R)
        direct01 = sb("direct01", [P, N])
        logit01 = sb("logit01", [P, B])
        logit2 = sb("logit2", [P, CB + B])
        idx = sb("idx", [P, F], I32)
        emb = sb("emb", [P, F * D])
        stage = sb("stage", [P, CHUNKS, D // 2, CB])
        ident = sb("ident", [P, P])
        w_plain = [sb(f"w{n}_plain", [P, len(PLAIN_TILES[n]), S]) for n in SPLITS]
        w_hi = [sb(f"w{n}_hi", [P, W_SPLITS[n], S], F32R) for n in SPLITS]
        w_lo = [sb(f"w{n}_lo", [P, W_SPLITS[n], S], F32R) for n in SPLITS]
        columns = sb("columns", [P, COLUMNS])
        b0_sb, b1_sb, b2_sb = (columns[:, i:i + 1] for i in range(3))
        bt1_sb, bt2_sb, wt3_sb = (columns[:, i:j] for i, j in ((3, BT2), (BT2, WT3), (WT3, COLUMNS)))
        def early_part(first, tiles):
            return x0_pairs[1][:, first:first + 4, :].rearrange("p a n -> p (a n)")[:, 0:tiles * S]

        w0_raw, w0_swapped = early_part(0, T0)[0:R0], early_part(4, T0)[0:R0]
        w_raw = [w0_raw[:, 0:W_SPLITS[0] * S], early_part(8, W_SPLITS[1]), early_part(12, W_SPLITS[2])]
        def top_part(first, n):
            return x0_pairs[0][:, first:first + n, :].rearrange("p a n -> p (a n)")

        wt1a_sb, wt1b_sb, wt1c_sb = top_part(0, 1), top_part(1, 1), top_part(2, 1)[0:DENSE_ROWS]
        wt2_sb = top_part(3, 2).rearrange("p (t n) -> p t n", n=H2)
        dense_sb = top_part(5, 4)[0:DENSE_ROWS]
        h2_sb = top_part(9, 4).rearrange("p (i m n) -> p i m n", i=2, n=NB)
        y_sb = top_part(13, 4)[0:1]
        h1_sb = x0_diag[:].rearrange("p (i m) n -> p i m n", i=2)
        dense_parts = pair_hi[0:DENSE_ROWS].rearrange("p a b n -> p (a b n)")
        wt1c_parts = half_parts[0:DENSE_ROWS]

        z = [ps("z0"), ps("z1"), ps("z2")]
        turned = [ps("turned0"), ps("turned1")]
        xk0 = ps("xk0")
        xk1, xk2 = ps("xk1"), ps("xk2")
        top = [z[0], z[1], xk0, xk1, xk2, z[2]]

        swapped_in = sem("swapped_in")
        raw_in = sem("raw_in")
        w0_summed = sem("w0_summed")
        w_hi_ready = sem("w_hi_ready")
        w_split = sem("w_split")
        weights_in = sem("weights_in")
        top_weights_in = sem("top_weights_in")
        ident_zero = sem("ident_zero")
        ident_ready = sem("ident_ready")
        idx_in = sem("idx_in")
        waits_held = sem("waits_held")
        gathered = sem("gathered")
        turned_ready = sem("turned_ready")
        stage_ready = sem("stage_ready")
        xt_stored = sem("xt_stored")
        x0_diag_in = sem("x0_diag_in")
        x0_pairs_in = [sem(f"x0_pairs_in{i}") for i in range(2)]
        prod_ready = sem("prod_ready")
        hi_ready = sem("hi_ready")
        lo_ready = [sem("lo0_ready"), sem("lo1_ready"), sem("lo2_ready")]
        slot_free = sem("slot_free")
        xk0_ready = sem("xk0_ready")
        xk_ready = [sem("xk1_ready"), sem("xk2_ready")]
        direct01_ready = sem("direct01_ready")
        direct2_ready = sem("direct2_ready")
        summed01 = sem("summed01")
        summed2 = sem("summed2")
        h_ready = sem("h_ready")
        h_relu = sem("h_relu")
        top_hi_ready = sem("top_hi_ready")
        top_lo_ready = sem("top_lo_ready")
        y_stored = sem("y_stored")

        def low_part(engine, layer, pos, at, n, pair):
            held, rows = prod[:, pos % RING], P if layer else R0
            if n == 1:
                engine.tensor_tensor(half_parts[HALF:P], held[HALF:P, at, :],
                                     half_parts[HALF:P].bitcast(F32),
                                     ALU.subtract).then_inc(lo_ready[layer], 1)
            else:
                engine.tensor_tensor(pair_lo[0:rows, pair % PAIR_RING], held[0:rows, at:at + 2, :],
                                     pair_hi[0:rows, pair % PAIR_RING].bitcast(F32),
                                     ALU.subtract).then_inc(lo_ready[layer], 1)

        block = ctx.enter_context(nc.Block())

        @block.sync
        def _(sp):
            sp.dma_start(w0_swapped, w0s).then_inc(swapped_in, 16)
            sp.dma_start(w0_raw, w0f).then_inc(swapped_in, 16)
            plain = [len(PLAIN_TILES[n]) for n in (1, 2)]
            for raw, w, first in zip(w_raw[1:], (w1, w2), plain):
                sp.dma_start(raw.rearrange("p (t s) -> p t s", s=S), w[:, first:]).then_inc(raw_in, 16)
            loads = [(w_plain[1][:], w1[:, 0:plain[0]]), (w_plain[2][:], w2[:, 0:plain[1]]),
                     (columns[:], small)]
            assert len(loads) == WEIGHT_DMAS
            for dst, src in loads:
                sp.dma_start(dst, src).then_inc(weights_in, 16)

            sums_done = sp.alloc_register("sums_done")
            slots_done = sp.alloc_register("slots_done")

            def ahead(value):
                return value if isinstance(value, int) else sp.snap(value)

            def store_group(bt):
                first = ahead(bt * (P * D))
                sp.wait_ge(stage_ready, 2 * (bt + 1))
                cols = xt[:, bass.ds(first, P * D)].rearrange(
                    "f (c e n) -> f c e n", c=CHUNKS, e=2)
                for half in range(2):
                    src = stage[half:2 * F:2].rearrange("p c d b -> p c (d b)")
                    sp.dma_start(cols[0:F, :, half, :], src).then_inc(xt_stored, 16)
                    sp.dma_start(cols[F:F + WRAP, :, half, :], src[0:WRAP]).then_inc(xt_stored, 16)

            def load_chunk(bt, c):
                first = ahead(bt * (P * D) + c * N)
                sums = bt * CHUNKS + c
                slots = sums * SLC - SLC + SL0 + 1
                if not isinstance(bt, int):
                    sp.reg_mov(sums_done, sums)
                    sp.reg_mov(slots_done, slots)
                    sums, slots = sums_done, slots_done
                if c == 0:
                    sp.wait_ge(xt_stored, 16 * ST_DMAS * (bt + 1))
                if not (isinstance(bt, int) and bt == c == 0):
                    sp.wait_ge(summed2, sums)
                chunk = xt[:, bass.ds(first, N)]
                for i in range(DIAG):
                    rows = slice(i * F, (i + 1) * F)
                    shifted = bass.AP(tensor=chunk.tensor, offset=chunk[i:i + F].offset,
                                      ap=[[COLS, F], [DIAG * COLS, T0], [1, N]])
                    sp.dma_start(x0_diag[rows, 0:T0, :], shifted).then_inc(x0_diag_in, 16)
                    sp.dma_start(x0_diag[rows, T0, :], chunk[0:F]).then_inc(x0_diag_in, 16)
                if not (isinstance(bt, int) and bt == c == 0):
                    sp.wait_ge(prod_ready, slots)
                buf, loaded = x0_pairs[c % 2], x0_pairs_in[c % 2]
                for half in range(2):
                    src = chunk[half:half + F - 1].rearrange("(t two) n -> t two n", two=2)[:, 0, :]
                    sp.dma_start(buf[half * HALF:(half + 1) * HALF, 0:TX - 1, :],
                                 src.partition_broadcast(HALF)).then_inc(loaded, 16)
                src = chunk[F - 1:F].rearrange("o n -> (o n)")
                sp.dma_start(buf[:, TX - 1, :], src.partition_broadcast(P)).then_inc(loaded, 16)

            def load_top():
                sp.wait_ge(prod_ready, (GROUPS * CHUNKS - 1) * SLC + SL0 + 1)
                loads = [
                    (wt1a_sb[0:HALF], wt1[HALF:P]), (wt1a_sb[HALF:P], wt1[0:HALF]),
                    (wt1b_sb, wt1[P:2 * P]), (wt1c_sb, wt1c),
                    (wt2_sb, wt2.rearrange("(t p) n -> p t n", p=P)), (dense_sb, dense_t),
                ]
                assert len(loads) == TOP_DMAS
                for dst, src in loads:
                    sp.dma_start(dst, src).then_inc(top_weights_in, 16)

            store_group(0)
            sp.wait_ge(w0_summed, 2)
            sp.wait_ge(w_split, 3)
            load_chunk(0, 0)

            def group(bt, last):
                for c in range(CHUNKS):
                    if c == 2 and not last:
                        store_group(bt + 1)
                    if c < CHUNKS - 1:
                        load_chunk(bt, c + 1)
                    elif not last:
                        load_chunk(bt + 1, 0)
                    else:
                        load_top()

            with sp.Fori(0, GROUPS - 1) as bt:
                group(bt, False)
            group(GROUPS - 1, True)
            sp.wait_ge(h_relu, TOP_STEPS)
            sp.dma_start(out, y_sb).then_inc(y_stored, 16)
            sp.wait_ge(y_stored, 16)

        @block.gpsimd
        def _(pool):
            nc.gpsimd.memset(ident[:], 0.0).then_inc(ident_zero, 1)
            pool.wait_ge(ident_zero, 1)
            nc.gpsimd.affine_select(out=ident[:], in_=ident[:], compare_op=ALU.not_equal, fill=1.0,
                                    base=0, pattern=[[-1, P]], channel_multiplier=1
                                    ).then_inc(ident_ready, 1)

            def load_indices(bt):
                pool.dma_start(idx[:], ids[bass.ds(bt * P, P), :]).then_inc(idx_in, 16)

            def start_group(bt, first):
                pool.wait_ge(idx_in, 16 * (bt + 1))
                if not first:
                    pool.wait_ge(turned_ready, 2 * bt)
                    pool.sem_inc(waits_held, 1)

            def gather(fields):
                for f in fields:
                    nc.gpsimd.indirect_dma_start(
                        out=emb[:, f * D:(f + 1) * D], out_offset=None, in_=tables[f],
                        in_offset=bass.IndirectOffsetOnAxis(ap=idx[:, f:f + 1], axis=0),
                    ).then_inc(gathered, 16)

            def group(bt, fields_at):
                pair = PAIRS[0]
                fields_done = 0 if isinstance(bt, int) and bt == GROUPS - 1 else GATHERS_AHEAD
                for c in range(CHUNKS):
                    chunk = bt * CHUNKS + c
                    pool.wait_ge(gathered, 16 * ((bt + 1) * F + fields_done))
                    fields = fields_at[c]
                    if fields and fields[0] == 0:
                        pool.sem_inc(waits_held, 1)
                        load_indices(bt + 2)
                    pair, pos = pair + PAIRS[1], SL0 + c * SLC + SLX
                    split = len(SPLITS[0]) + chunk * SPLITS_C + len(SPLITS[1])
                    if not (isinstance(bt, int) and bt == GROUPS - 1 and c == CHUNKS - 1):
                        pair, pos, split = pair + PAIRS[0], pos + SL0, split + len(SPLITS[0])
                    for i, (k, at, n) in enumerate(SPLITS[2]):
                        pool.wait_ge(hi_ready, split + i + 1)
                        if i > 0:
                            pool.wait_ge(lo_ready[2], chunk * len(SPLITS[2]) + i)
                        low_part(nc.gpsimd, 2, pos + k, at, n, pair)
                        pair += n == 2
                    if fields and fields[0] == 0:
                        start_group(bt + 2, False)
                    gather(fields)
                    fields_done += len(fields)

            load_indices(0)
            start_group(0, True)
            gather(range(F))
            pool.wait_ge(gathered, 16 * F)
            load_indices(1)
            start_group(1, False)
            gather(range(0, GATHERS_AHEAD))
            with pool.Fori(0, GROUPS - 2) as bt:
                group(bt, GATHERS_AT)
            group(GROUPS - 2, GATHERS_AT[:1] + [[]] * (CHUNKS - 1))
            group(GROUPS - 1, [[]] * CHUNKS)

        @block.vector
        def _(dve):
            dve.sem_inc(slot_free, RING)
            dve.wait_ge(swapped_in, 32)
            split = W_SPLITS[0] * S
            nc.vector.tensor_tensor(w_raw[0], w_raw[0], w0_swapped[:, 0:split], ALU.add
                                    ).then_inc(w0_summed, 1)
            nc.vector.tensor_tensor(w_plain[0][0:R0].rearrange("p t s -> p (t s)"), w0_raw[:, split:],
                                    w0_swapped[:, split:], ALU.add).then_inc(w0_summed, 1)
            for i, n in enumerate(W_ORDER):
                rows = w_raw[n].shape[0]
                dve.wait_ge(w_hi_ready, i + 1)
                nc.vector.tensor_tensor(w_lo[n][0:rows].rearrange("p t s -> p (t s)"), w_raw[n],
                                        w_hi[n][0:rows].bitcast(F32).rearrange("p t s -> p (t s)"),
                                        ALU.subtract).then_inc(w_split, 1)

            def product(slot, pos, a, xk):
                rows, n = a.shape[0], a.shape[1]
                dve.wait_ge(slot_free, slot + 1)
                nc.vector.tensor_tensor(prod[0:rows, pos % RING, 0:n, :], a,
                                        xk.unsqueeze(1).broadcast_to([rows, n, N]),
                                        ALU.mult).then_inc(prod_ready, 1)

            def products(steps, split, pair, next_chunk):
                late = []
                for n, k, copies, xk, slot, pos in steps:
                    if n == k == 0:
                        dve.wait_ge(xk0_ready, next_chunk + 1)
                    first, rows, tiles = (FIRST_TILE[k], P, TX) if n else (L0_FIRST[k], R0, T0)
                    product(slot, pos, copies[0:rows, first:min(first + QUAD, tiles), :], xk[0:rows])
                    if (n, k) != (1, 1):
                        for item in late:
                            split, pair = subtract(item, split, pair)
                        late = []
                    late += [(n, pos, at, m) for at_slot, at, m in SPLITS[n] if at_slot == k]
                for item in late:
                    split, pair = subtract(item, split, pair)

            def subtract(item, split, pair):
                n, pos, at, m = item
                dve.wait_ge(hi_ready, split + 1)
                low_part(nc.vector, n, pos, at, m, pair)
                return split + 1, pair + (m == 2)

            def sum01(chunk):
                dve.wait_ge(direct01_ready, 2 * chunk + 2)
                nc.vector.tensor_reduce(logit01[:, bass.ds(chunk * CB, CB)],
                                        direct01[:].rearrange("p (d b) -> p b d", b=CB),
                                        AXIS.X, ALU.add).then_inc(summed01, 1)

            def sum2(chunk):
                dve.wait_ge(direct2_ready, chunk + 1)
                nc.vector.tensor_reduce(logit2[:, bass.ds(chunk * CB, CB)],
                                        z[2][:].rearrange("p (d b) -> p b d", b=CB),
                                        AXIS.X, ALU.add).then_inc(summed2, 1)

            def layer(n, copies, xk, slot, pos):
                return [(n, k, copies, xk, slot + k, pos + k) for k in range(SLX if n else SL0)]

            products(layer(0, x0_diag, xk0, 0, 0), 0, 0, 0)
            nc.vector.memset(z[2][:], 0.0).then_inc(summed2, 1)

            def group(bt, last):
                pair = PAIRS[0]
                for c in range(CHUNKS):
                    chunk = bt * CHUNKS + c
                    slot, pos = SL0 + chunk * SLC, SL0 + c * SLC
                    split = len(SPLITS[0]) + chunk * SPLITS_C
                    copies = x0_pairs[c % 2]
                    dve.wait_ge(x0_pairs_in[c % 2],
                                16 * X0_PAIRS_DMAS * (bt * (CHUNKS // 2) + c // 2 + 1))
                    dve.wait_ge(xk_ready[0], chunk + 1)
                    steps = layer(1, copies, xk1, slot, pos)
                    pair_after = pair + PAIRS[1]
                    if not (last and c == CHUNKS - 1):
                        steps += layer(0, x0_diag, xk0, slot + SLX, pos + SLX)
                        pair_after += PAIRS[0]
                    products(steps, split, pair, chunk + 1)
                    slot, pos = slot + len(steps), pos + len(steps)
                    sum2(chunk)
                    dve.wait_ge(xk_ready[1], chunk + 1)
                    for k in range(SLX):
                        product(slot + k, pos + k, copies[:, FIRST_TILE[k]:FIRST_TILE[k] + QUAD, :],
                                xk2[:])
                        if k == 1:
                            sum01(chunk)
                    pair = pair_after + PAIRS[2]

            with dve.Fori(0, GROUPS - 1) as bt:
                group(bt, False)
            group(GROUPS - 1, True)
            dve.wait_ge(top_hi_ready, 1)
            rows = slice(DENSE_ROWS - DENSE, DENSE_ROWS)
            nc.vector.tensor_tensor(wt1c_parts[rows], wt1c_sb[rows], wt1c_parts[rows].bitcast(F32),
                                    ALU.subtract).then_inc(top_lo_ready, 1)
            for n in range(B // NB):
                if n == 1:
                    sum2(GROUPS * CHUNKS)
                dve.wait_ge(top_hi_ready, n + 2)
                rows, cols = slice(32, 64), slice(n * NB, (n + 1) * NB)
                nc.vector.tensor_tensor(dense_parts[rows, cols], dense_sb[rows, cols],
                                        dense_parts[rows, cols].bitcast(F32),
                                        ALU.subtract).then_inc(top_lo_ready, 1)

        @block.scalar
        def _(act):
            def fill_stage(bt):
                if not (isinstance(bt, int) and bt == 0):
                    act.wait_ge(xt_stored, 16 * ST_DMAS * bt)
                for q in range(2):
                    act.wait_ge(turned_ready, 2 * bt + q + 1)
                    nc.scalar.copy(stage[0:2 * F, :, 4 * q:4 * q + 4, :].rearrange("p c d b -> p d c b"),
                                   turned[q][0:2 * F].rearrange("p (d c b) -> p d c b", d=4, c=CHUNKS)
                                   ).then_inc(stage_ready, 1)

            def round_splits(splits, rows, slot, pos, pair, held_by):
                for k, at, n in splits:
                    act.wait_ge(prod_ready, slot + k + 1)
                    held = prod[0:rows, (pos + k) % RING]
                    if n == 1:
                        nc.scalar.copy(half_parts[:], held[:, at, :]).then_inc(hi_ready, 1)
                    else:
                        act.wait_ge(slot_free, RING + held_by[-PAIR_RING] + 1)
                        nc.scalar.copy(pair_hi[0:rows, pair % PAIR_RING], held[:, at:at + 2, :]
                                       ).then_inc(hi_ready, 1)
                        held_by.append(slot + k)
                        pair += 1
                return pair

            def hand_on(layer, xk, b, slots):
                act.wait_ge(slot_free, RING + slots)
                nc.scalar.activation(xk[0:HALF], z[layer][0:HALF], ACT.Relu, bias=b[0:HALF])
                nc.scalar.activation(xk[HALF:P], z[layer][0:HALF], ACT.Relu, bias=b[0:HALF]
                                     ).then_inc(xk_ready[layer], 1)

            def copy_xk0(chunk):
                act.wait_ge(x0_diag_in, 16 * X0_DIAG_DMAS * (chunk + 1))
                nc.scalar.copy(xk0[0:R0], x0_diag[0:R0, T0, :]).then_inc(xk0_ready, 1)

            def direct_0():
                nc.scalar.activation(direct01[HALF:P], z[0][HALF:P], ACT.Relu, bias=b0_sb[HALF:P]
                                     ).then_inc(direct01_ready, 1)

            def direct_2(chunk, slots):
                act.wait_ge(slot_free, RING + slots)
                act.wait_ge(summed2, chunk + 1)
                nc.scalar.activation(z[2][:], z[2][:], ACT.Relu, bias=b2_sb
                                     ).then_inc(direct2_ready, 1)

            act.wait_ge(raw_in, 16 * RAW_DMAS)
            for n in W_ORDER:
                if n == 0:
                    act.wait_ge(w0_summed, 1)
                nc.scalar.copy(w_hi[n][0:w_raw[n].shape[0]].rearrange("p t s -> p (t s)"), w_raw[n]
                               ).then_inc(w_hi_ready, 1)
            act.wait_ge(weights_in, 16 * WEIGHT_DMAS)
            fill_stage(0)
            copy_xk0(0)
            assert len(SPLITS[0]) == 1
            (k, at, n), = SPLITS[0]
            act.wait_ge(prod_ready, k + 1)
            nc.scalar.copy(pair_hi[0:R0, 0], prod[0:R0, k, at:at + n, :]).then_inc(hi_ready, 1)
            hand_on(0, xk1, b0_sb, SL0)
            direct_0()

            def group(bt, last):
                pair = PAIRS[0]
                before = SL0 + bt * CHUNKS * SLC
                held_by = [before - SLX + k for k, _, n in SPLITS[2] if n == 2]
                for c in range(CHUNKS):
                    chunk = bt * CHUNKS + c
                    slot, pos = SL0 + chunk * SLC, SL0 + c * SLC
                    pair = round_splits(SPLITS[1][:EARLY[1]], P, slot, pos, pair, held_by)
                    direct_2(chunk, slot)
                    if not (last and c == CHUNKS - 1):
                        copy_xk0(chunk + 1)
                    pair = round_splits(SPLITS[1][EARLY[1]:], P, slot, pos, pair, held_by)
                    slot, pos = slot + SLX, pos + SLX
                    if not (last and c == CHUNKS - 1):
                        pair = round_splits(SPLITS[0], R0, slot, pos, pair, held_by)
                    hand_on(1, xk2, b1_sb, slot)
                    nc.scalar.activation(direct01[0:HALF], z[1][HALF:P], ACT.Relu, bias=b1_sb[HALF:P]
                                         ).then_inc(direct01_ready, 1)
                    if c == 1 and not last:
                        fill_stage(bt + 1)
                    if last and c == CHUNKS - 1:
                        round_splits(SPLITS[2], P, slot, pos, pair, held_by)
                    else:
                        slot, pos = slot + SL0, pos + SL0
                        pair = round_splits(SPLITS[2][:EARLY[2]], P, slot, pos, pair, held_by)
                        hand_on(0, xk1, b0_sb, slot)
                        act.wait_ge(summed01, chunk + 1)
                        direct_0()
                        pair = round_splits(SPLITS[2][EARLY[2]:], P, slot, pos, pair, held_by)

            with act.Fori(0, GROUPS - 1) as bt:
                group(bt, False)
            group(GROUPS - 1, True)
            act.wait_ge(top_weights_in, 16 * TOP_DMAS)
            act.wait_ge(slot_free, RING + SLC * CHUNKS * GROUPS)
            nc.scalar.copy(wt1c_parts, wt1c_sb).then_inc(top_hi_ready, 1)
            for n in range(B // NB):
                cols = slice(n * NB, (n + 1) * NB)
                nc.scalar.copy(dense_parts[:, cols], dense_sb[:, cols]).then_inc(top_hi_ready, 1)
                if n == 0:
                    direct_2(GROUPS * CHUNKS, SLC * CHUNKS * GROUPS)

            for step, (kind, n, m) in enumerate(TOP_ORDER):
                act.wait_ge(h_ready, step + 1)
                acc = top[step % len(top)]
                if kind == "h1":
                    nc.scalar.activation(h1_sb[:, n % 2, m, :], acc[:], ACT.Relu,
                                         bias=bt1_sb[:, m:m + 1]).then_inc(h_relu, 1)
                elif kind == "h2":
                    nc.scalar.activation(h2_sb[:, n % 2, m, :], acc[:], ACT.Relu,
                                         bias=bt2_sb[:, m:m + 1]).then_inc(h_relu, 1)
                else:
                    nc.scalar.copy(y_sb[:, n * NB:(n + 1) * NB], acc[0:1, :]).then_inc(h_relu, 1)

        @block.tensor
        def _(pe):
            def transpose_group(bt):
                pe.wait_ge(gathered, 16 * F * (bt + 1))
                if not (isinstance(bt, int) and bt == 0):
                    pe.wait_ge(stage_ready, 2 * bt)
                for d in range(D // 2):
                    ins = nc.tensor.transpose(turned[d // 4][0:2 * F, d % 4 * P:(d % 4 + 1) * P],
                                              emb[:, d:F * D:D // 2], ident[:])
                    if d % 4 == 3:
                        ins.then_inc(turned_ready, 1)

            def layer(n, slot, pos, split, pair):
                whole, hi, lo, splits = w_plain[n], w_hi[n], w_lo[n], SPLITS[n]
                first_tile = FIRST_TILE if n else L0_FIRST
                last_slot = len(first_tile) - 1
                for k, t in enumerate(first_tile):
                    held = prod[:, (pos + k) % RING]
                    here = [s for s in splits if s[0] == k]
                    places = range(QUAD if n else min(QUAD, T0 - t))
                    plain = [i for i in places if not any(at <= i < at + m for _, at, m in here)]
                    pe.wait_ge(prod_ready, slot + k + 1)
                    for i in plain:
                        rows = P if n else R0_LAST if t + i == T0 - 1 else R0
                        w = whole[0:rows, PLAIN_TILES[n].index(t + i), :]
                        ins = nc.tensor.matmul(z[n][:], w, held[0:rows, i, :],
                                               start=(k == 0 and i == plain[0]),
                                               stop=(k == last_slot and not here and i == plain[-1]))
                    for s in here:
                        _, at, m = s
                        pe.wait_ge(lo_ready[n], split + 1)
                        if m == 1:
                            terms = [(lo[:, W_SPLITS[n] - 1, :], half_parts[:]),
                                     (hi[:, W_SPLITS[n] - 1, :], half_parts[:])]
                        else:
                            terms = []
                            for i in range(2):
                                j = SPLIT_TILES[n].index(t + at + i)
                                rows = P if n else R0
                                p_hi = pair_hi[0:rows, pair % PAIR_RING, i, :]
                                p_lo = pair_lo[0:rows, pair % PAIR_RING, i, :]
                                w_h, w_l = hi[0:rows, j, :], lo[0:rows, j, :]
                                terms += [(w_l, p_hi), (w_h, p_lo), (w_h, p_hi)]
                            pair += 1
                        for i, (w, x) in enumerate(terms):
                            ins = nc.tensor.matmul(z[n][:], w, x, start=False,
                                                   stop=(k == last_slot and s is here[-1]
                                                         and i == len(terms) - 1))
                        split = split + 1
                    ins.then_inc(slot_free, 1)
                return pair

            pe.wait_ge(ident_ready, 1)
            transpose_group(0)
            pe.wait_ge(w0_summed, 2)
            pe.wait_ge(w_split, 3)
            pe.wait_ge(weights_in, 16 * WEIGHT_DMAS)
            layer(0, 0, 0, 0, 0)

            def group(bt, last):
                pair = PAIRS[0]
                for c in range(CHUNKS):
                    chunk = bt * CHUNKS + c
                    slot, pos = SL0 + chunk * SLC, SL0 + c * SLC
                    pe.wait_ge(direct01_ready, 2 * chunk + 1)
                    pair = layer(1, slot, pos, chunk * len(SPLITS[1]), pair)
                    slot, pos = slot + SLX, pos + SLX
                    if c == 1 and not last:
                        transpose_group(bt + 1)
                    if not (last and c == CHUNKS - 1):
                        pair = layer(0, slot, pos, (chunk + 1) * len(SPLITS[0]), pair)
                        slot, pos = slot + SL0, pos + SL0
                    pe.wait_ge(summed2, chunk + 2)
                    pair = layer(2, slot, pos, chunk * len(SPLITS[2]), pair)

            with pe.Fori(0, GROUPS - 1) as bt:
                group(bt, False)
            group(GROUPS - 1, True)

            pe.wait_ge(top_weights_in, 16 * TOP_DMAS)
            pe.wait_ge(summed01, GROUPS * CHUNKS)
            pe.wait_ge(summed2, GROUPS * CHUNKS + 1)
            pe.wait_ge(direct01_ready, 2 * GROUPS * CHUNKS)
            for step, (kind, n, m) in enumerate(TOP_ORDER):
                acc = top[step % len(top)]
                if step == len(top) - 1:
                    pe.wait_ge(summed2, GROUPS * CHUNKS + 2)
                if step >= len(top):
                    pe.wait_ge(h_relu, step - len(top) + 1)
                cols, rows = slice(n * NB, (n + 1) * NB), slice(m * P, (m + 1) * P)
                if kind == "h1":
                    terms = [(wt1a_sb[:, rows], logit01[:, n * NB:(n + 1) * NB]),
                             (wt1b_sb[:, rows], logit2[:, CB + n * NB:CB + (n + 1) * NB]),
                             (wt1c_parts[:, rows], dense_parts[:, cols])]
                elif kind == "h2":
                    pe.wait_ge(h_relu, last_h1(n))
                    terms = [(wt2_sb[:, k, rows], h1_sb[:, n % 2, k, :]) for k in range(H1 // P)]
                else:
                    pe.wait_ge(h_relu, step)
                    terms = [(wt3_sb[:, k:k + 1], h2_sb[:, n % 2, k, :]) for k in range(H2 // P)]
                for k, (w, x) in enumerate(terms):
                    if kind == "h1" and k == len(terms) - 1:
                        pe.wait_ge(top_lo_ready, n + 2)
                    ins = nc.tensor.matmul(acc[0:w.shape[1]], w, x, start=(k == 0),
                                           stop=(k == len(terms) - 1))
                ins.then_inc(h_ready, 1)


def kernel(**inputs):
    import numpy as np
    import concourse.bacc as bacc
    from concourse.bass_utils import run_bass_kernel_spmd

    raw = {k: np.asarray(v) for k, v in inputs.items()}
    h = np.arange(F)
    w0 = raw["L0_rec_w0"]
    w0f = np.zeros((R0, T0, S), w0.dtype)
    w0s = np.zeros((R0, T0, S), w0.dtype)
    for j in range(F // 2 + 1):
        t, rows = j // DIAG, slice(j % DIAG * F, (j % DIAG + 1) * F)
        w0f[rows, t] = w0[h, (h + j) % F]
        if j > 0:
            w0s[rows, t] = w0[(h + j) % F, h]

    def by_tile(w, n):
        rows = w.reshape(F * HALF, S)
        tiles = [rows[t * P:(t + 1) * P] for t in PLAIN_TILES[n] + SPLIT_TILES[n]]
        tiles.append(np.concatenate([rows[(TX - 1) * P:]] * 2))
        return np.ascontiguousarray(np.stack(tiles, axis=1))

    def thrice(rows):
        out = np.zeros((DENSE_ROWS, rows.shape[1]), rows.dtype)
        for first in (0, 32, 64):
            out[first:first + DENSE] = rows
        return out

    arrays = {f"in_tbl_{f}": raw[f"tbl_{f}"] for f in range(F)}
    arrays.update(
        in_ids=raw["ids"],
        in_dense_t=thrice(raw["dense_ctx"].T),
        in_wt1c=thrice(raw["W_top1"][2 * P:]),
        in_w0f=w0f.reshape(R0, T0 * S),
        in_w0s=w0s.reshape(R0, T0 * S),
        in_w1=by_tile(raw["L0_rec_w1"], 1),
        in_w2=by_tile(raw["L0_rec_w2"], 2),
        in_small=np.concatenate([raw[k].reshape(-1, P) for k in (
            "L0_rec_b0", "L0_rec_b1", "L0_rec_b2", "b_top1", "b_top2", "W_top3")]).T.copy(),
        in_wt1=raw["W_top1"],
        in_wt2=raw["W_top2"],
    )
    nc = bacc.Bacc("TRN2", target_bir_lowering=False, num_devices=1)
    aps = {k: nc.dram_tensor(k, a.shape, mybir.dt.from_np(a.dtype), kind="ExternalInput").ap()
           for k, a in arrays.items()}
    out = nc.dram_tensor("out_y", (1, B), F32, kind="ExternalOutput").ap()
    names = ["ids", "dense_t", "w0f", "w0s", "w1", "w2", "small", "wt1", "wt1c", "wt2"]
    build(nc, [aps[f"in_tbl_{f}"] for f in range(F)], *(aps["in_" + k] for k in names), out)
    r = run_bass_kernel_spmd(nc, [arrays], core_ids=[0])
    return r.results[0]["out_y"].reshape(B, 1)
```
